# Optimizing a Trainium2 kernel written in Bass

```python
import numpy as np
import jax
import jax.numpy as jnp

def _softmax(x, axis=-1):
    return jax.nn.softmax(x, axis=axis)

def _gelu(x):
    return jax.nn.gelu(x, approximate=True)

def _silu(x):
    return jax.nn.silu(x)

def _sigmoid(x):
    return jax.nn.sigmoid(x)

def _layernorm(x, axis=-1, eps=1e-05):
    m = jnp.mean(x, axis=axis, keepdims=True)
    v = jnp.var(x, axis=axis, keepdims=True)
    return (x - m) / jnp.sqrt(v + eps)

def _scatter_add(tgt, idx, src, axis=0):
    return tgt.at[idx].add(src)

def _segment_sum(src, seg, n):
    return jax.ops.segment_sum(src, seg, n)
kernel_name = 'mk_cond_seq_d4_seqx_r8_38a781'

def setup_inputs(seed: int=0):
    np.random.seed(seed)
    _w = jnp.asarray

    def _rec_inputs():
        import jax
        import jax.numpy as jnp
        _rk = jax.random.key(seed)
        x = 1.648e-05 + 1 * jax.random.normal(jax.random.fold_in(_rk, 1), (32, 128, 144), jnp.float32)
        _lenS = 128 - jax.random.randint(jax.random.fold_in(_rk, 7), (32,), 0, max(1, 128 // 4) + 1, jnp.int32)
        _lenS2 = 128 - jax.random.randint(jax.random.fold_in(_rk, 8), (32,), 0, max(1, 128 // 4) + 1, jnp.int32)
        cond_1152 = 0.00914911 + 1.00357 * jax.random.normal(jax.random.fold_in(_rk, 11), (32, 144), jnp.float32)
        return (x, cond_1152)
    x, cond_1152 = _rec_inputs()

    def _L0_cond_setup():
        import jax, jax.numpy as jnp
        import numpy as np
        NUM_HEADS = 16
        NUM_EXPERTS = 4
        TOP_K = 2
        LN_EPS = 1e-06

        def _ln(h):
            mu = jnp.mean(h, axis=-1, keepdims=True)
            var = jnp.var(h, axis=-1, keepdims=True)
            return (h - mu) * jax.lax.rsqrt(var + LN_EPS)

        def _modulate(h, shift, scale):
            return h * (1.0 + scale[:, None, :]) + shift[:, None, :]
        key = jax.random.key(seed)
        ks = jax.random.split(key, 12)
        B, N, C = (8, 128, 144)
        H = 4 * C
        E = NUM_EXPERTS
        s = 0.02
        return {'x': jax.random.normal(ks[0], (B, N, C), jnp.float32), 'c': jax.random.normal(ks[1], (B, C), jnp.float32), 'w_adaln': jax.random.normal(ks[2], (C, 6 * C), jnp.float32) * s, 'b_adaln': jnp.zeros((6 * C,), jnp.float32), 'w_qkv': jax.random.normal(ks[3], (C, 3 * C), jnp.float32) * s, 'b_qkv': jnp.zeros((3 * C,), jnp.float32), 'w_proj': jax.random.normal(ks[4], (C, C), jnp.float32) * s, 'b_proj': jnp.zeros((C,), jnp.float32), 'w_gate': jax.random.normal(ks[5], (C, E), jnp.float32) * s, 'w1': jax.random.normal(ks[6], (E, C, H), jnp.float32) * s, 'b1': jnp.zeros((E, H), jnp.float32), 'w2': jax.random.normal(ks[7], (E, H, C), jnp.float32) * s, 'b2': jnp.zeros((E, C), jnp.float32)}
    _L0_cond_all = _L0_cond_setup()
    _L0_cond_in = {k: v for k, v in _L0_cond_all.items() if k in ('w_adaln', 'b_adaln', 'w_qkv', 'b_qkv', 'w_proj', 'b_proj', 'w_gate', 'w1', 'b1', 'w2', 'b2')}
    del _L0_cond_all

    def _L1_cond_setup():
        import jax, jax.numpy as jnp
        import numpy as np
        B, L, C = (8, 128, 144)
        H = 16
        D = C // H
        FF = int(C * 4.0)
        EPS = 1e-06

        def _layernorm(x):
            mu = jnp.mean(x, axis=-1, keepdims=True)
            var = jnp.mean(jnp.square(x - mu), axis=-1, keepdims=True)
            return (x - mu) * jax.lax.rsqrt(var + EPS)

        def _modulate(x, shift, scale):
            return x * (1.0 + scale) + shift

        def _attention(h, W_qkv, b_qkv, W_proj, b_proj):
            b, l, c = h.shape
            qkv = h @ W_qkv + b_qkv
            qkv = qkv.reshape(b, l, 3, H, D)
            q, k, v = (qkv[:, :, 0], qkv[:, :, 1], qkv[:, :, 2])
            scale = D ** (-0.5)
            scores = jnp.einsum('blhd,bmhd->bhlm', q * scale, k)
            attn = jax.nn.softmax(scores, axis=-1)
            o = jnp.einsum('bhlm,bmhd->blhd', attn, v).reshape(b, l, c)
            return o @ W_proj + b_proj
        key = jax.random.key(seed)
        ks = jax.random.split(key, 12)
        s = 0.02
        return {'x': jax.random.normal(ks[0], (B, L, C), jnp.float32), 'c': jax.random.normal(ks[1], (B, 1, C), jnp.float32), 'W_qkv': jax.random.normal(ks[2], (C, 3 * C), jnp.float32) * s, 'b_qkv': jnp.zeros((3 * C,), jnp.float32), 'W_proj': jax.random.normal(ks[3], (C, C), jnp.float32) * s, 'b_proj': jnp.zeros((C,), jnp.float32), 'W_fc1': jax.random.normal(ks[4], (C, FF), jnp.float32) * s, 'b_fc1': jnp.zeros((FF,), jnp.float32), 'W_fc2': jax.random.normal(ks[5], (FF, C), jnp.float32) * s, 'b_fc2': jnp.zeros((C,), jnp.float32), 'W_ada': jax.random.normal(ks[6], (C, 6 * C), jnp.float32) * s, 'b_ada': jnp.zeros((6 * C,), jnp.float32)}
    _L1_cond_all = _L1_cond_setup()
    _L1_cond_in = {k: v for k, v in _L1_cond_all.items() if k in ('W_qkv', 'b_qkv', 'W_proj', 'b_proj', 'W_fc1', 'b_fc1', 'W_fc2', 'b_fc2', 'W_ada', 'b_ada')}
    del _L1_cond_all

    def _L2_cond_setup():
        import jax, jax.numpy as jnp
        import numpy as np
        DIM = 144
        HEADS = 16
        HEAD_DIM = DIM // HEADS
        HIDDEN = int(DIM * 4.0)
        EPS = 1e-12

        def rmsnorm(x, g, d):
            n = jnp.linalg.norm(x, axis=-1, keepdims=True)
            return x / jnp.maximum(n, EPS) * d ** 0.5 * g

        def modulate(x, scale, shift):
            return x * (1.0 + scale[:, None, :]) + shift[:, None, :]
        key = jax.random.key(seed)
        ks = jax.random.split(key, 12)
        B, N = (8, 128)
        s = 0.02
        return {'x': jax.random.normal(ks[0], (B, N, DIM), jnp.float32), 'c': jax.random.normal(ks[1], (B, DIM), jnp.float32), 'g1': jnp.ones((1,), jnp.float32), 'g2': jnp.ones((1,), jnp.float32), 'qkv_w': jax.random.normal(ks[2], (3 * DIM, DIM), jnp.float32) * s, 'qkv_b': jnp.zeros((3 * DIM,), jnp.float32), 'qg': jnp.ones((1,), jnp.float32), 'kg': jnp.ones((1,), jnp.float32), 'proj_w': jax.random.normal(ks[3], (DIM, DIM), jnp.float32) * s, 'proj_b': jnp.zeros((DIM,), jnp.float32), 'fc1_w': jax.random.normal(ks[4], (HIDDEN, DIM), jnp.float32) * s, 'fc1_b': jnp.zeros((HIDDEN,), jnp.float32), 'fc2_w': jax.random.normal(ks[5], (DIM, HIDDEN), jnp.float32) * s, 'fc2_b': jnp.zeros((DIM,), jnp.float32), 'ada_w': jax.random.normal(ks[6], (6 * DIM, DIM), jnp.float32) * s, 'ada_b': jnp.zeros((6 * DIM,), jnp.float32)}
    _L2_cond_all = _L2_cond_setup()
    _L2_cond_in = {k: v for k, v in _L2_cond_all.items() if k in ('g1', 'g2', 'qkv_w', 'qkv_b', 'qg', 'kg', 'proj_w', 'proj_b', 'fc1_w', 'fc1_b', 'fc2_w', 'fc2_b', 'ada_w', 'ada_b')}
    del _L2_cond_all

    def _L3_cond_setup():
        import jax, jax.numpy as jnp
        import numpy as np
        N, T, D, H = (32, 128, 144, 16)
        DH = D // H
        MLP = int(D * 4.0)
        EPS = 1e-06

        def _layernorm(x):
            m = jnp.mean(x, axis=-1, keepdims=True)
            v = jnp.var(x, axis=-1, keepdims=True)
            return (x - m) * jax.lax.rsqrt(v + EPS)

        def _modulate(x, shift, scale):
            return x * (1.0 + scale[:, None, :]) + shift[:, None, :]

        def _attention(x, qkv_w, qkv_b, proj_w, proj_b):
            n, t, d = x.shape
            scale = DH ** (-0.5)
            qkv = x @ qkv_w + qkv_b
            qkv = qkv.reshape(n, t, 3, H, DH)
            q, k, v = (qkv[:, :, 0], qkv[:, :, 1], qkv[:, :, 2])
            attn = jnp.einsum('nthd,ntkd->nthk', q * scale, k)
            attn = jax.nn.softmax(attn, axis=-1)
            out = jnp.einsum('nthk,ntkd->nthd', attn, v)
            out = out.transpose(0, 2, 1, 3).reshape(n, t, d)
            return out @ proj_w + proj_b

        def _mlp(x, fc1_w, fc1_b, fc2_w, fc2_b):
            h = jax.nn.gelu(x @ fc1_w + fc1_b, approximate=False)
            return h @ fc2_w + fc2_b
        key = jax.random.key(seed)
        ks = jax.random.split(key, 14)
        s = 0.02
        return {'x': jax.random.normal(ks[0], (N, T, D), jnp.float32), 'c': jax.random.normal(ks[1], (N, D), jnp.float32), 'qkv_w': jax.random.normal(ks[2], (D, 3 * D), jnp.float32) * s, 'qkv_b': jax.random.normal(ks[3], (3 * D,), jnp.float32) * s, 'proj_w': jax.random.normal(ks[4], (D, D), jnp.float32) * s, 'proj_b': jax.random.normal(ks[5], (D,), jnp.float32) * s, 'fc1_w': jax.random.normal(ks[6], (D, MLP), jnp.float32) * s, 'fc1_b': jax.random.normal(ks[7], (MLP,), jnp.float32) * s, 'fc2_w': jax.random.normal(ks[8], (MLP, D), jnp.float32) * s, 'fc2_b': jax.random.normal(ks[9], (D,), jnp.float32) * s, 'ada_w': jax.random.normal(ks[10], (D, 6 * D), jnp.float32) * s, 'ada_b': jax.random.normal(ks[11], (6 * D,), jnp.float32) * s}
    _L3_cond_all = _L3_cond_setup()
    _L3_cond_in = {k: v for k, v in _L3_cond_all.items() if k in ('qkv_w', 'qkv_b', 'proj_w', 'proj_b', 'fc1_w', 'fc1_b', 'fc2_w', 'fc2_b', 'ada_w', 'ada_b')}
    del _L3_cond_all
    return {'x': x, 'cond_1152': cond_1152, 'L0_cond_w_adaln': _L0_cond_in['w_adaln'], 'L0_cond_b_adaln': _L0_cond_in['b_adaln'], 'L0_cond_w_qkv': _L0_cond_in['w_qkv'], 'L0_cond_b_qkv': _L0_cond_in['b_qkv'], 'L0_cond_w_proj': _L0_cond_in['w_proj'], 'L0_cond_b_proj': _L0_cond_in['b_proj'], 'L0_cond_w_gate': _L0_cond_in['w_gate'], 'L0_cond_w1': _L0_cond_in['w1'], 'L0_cond_b1': _L0_cond_in['b1'], 'L0_cond_w2': _L0_cond_in['w2'], 'L0_cond_b2': _L0_cond_in['b2'], 'L1_cond_W_qkv': _L1_cond_in['W_qkv'], 'L1_cond_b_qkv': _L1_cond_in['b_qkv'], 'L1_cond_W_proj': _L1_cond_in['W_proj'], 'L1_cond_b_proj': _L1_cond_in['b_proj'], 'L1_cond_W_fc1': _L1_cond_in['W_fc1'], 'L1_cond_b_fc1': _L1_cond_in['b_fc1'], 'L1_cond_W_fc2': _L1_cond_in['W_fc2'], 'L1_cond_b_fc2': _L1_cond_in['b_fc2'], 'L1_cond_W_ada': _L1_cond_in['W_ada'], 'L1_cond_b_ada': _L1_cond_in['b_ada'], 'L2_cond_g1': _L2_cond_in['g1'], 'L2_cond_g2': _L2_cond_in['g2'], 'L2_cond_qkv_w': _L2_cond_in['qkv_w'], 'L2_cond_qkv_b': _L2_cond_in['qkv_b'], 'L2_cond_qg': _L2_cond_in['qg'], 'L2_cond_kg': _L2_cond_in['kg'], 'L2_cond_proj_w': _L2_cond_in['proj_w'], 'L2_cond_proj_b': _L2_cond_in['proj_b'], 'L2_cond_fc1_w': _L2_cond_in['fc1_w'], 'L2_cond_fc1_b': _L2_cond_in['fc1_b'], 'L2_cond_fc2_w': _L2_cond_in['fc2_w'], 'L2_cond_fc2_b': _L2_cond_in['fc2_b'], 'L2_cond_ada_w': _L2_cond_in['ada_w'], 'L2_cond_ada_b': _L2_cond_in['ada_b'], 'L3_cond_qkv_w': _L3_cond_in['qkv_w'], 'L3_cond_qkv_b': _L3_cond_in['qkv_b'], 'L3_cond_proj_w': _L3_cond_in['proj_w'], 'L3_cond_proj_b': _L3_cond_in['proj_b'], 'L3_cond_fc1_w': _L3_cond_in['fc1_w'], 'L3_cond_fc1_b': _L3_cond_in['fc1_b'], 'L3_cond_fc2_w': _L3_cond_in['fc2_w'], 'L3_cond_fc2_b': _L3_cond_in['fc2_b'], 'L3_cond_ada_w': _L3_cond_in['ada_w'], 'L3_cond_ada_b': _L3_cond_in['ada_b']}

def reference(x, cond_1152, L0_cond_w_adaln, L0_cond_b_adaln, L0_cond_w_qkv, L0_cond_b_qkv, L0_cond_w_proj, L0_cond_b_proj, L0_cond_w_gate, L0_cond_w1, L0_cond_b1, L0_cond_w2, L0_cond_b2, L1_cond_W_qkv, L1_cond_b_qkv, L1_cond_W_proj, L1_cond_b_proj, L1_cond_W_fc1, L1_cond_b_fc1, L1_cond_W_fc2, L1_cond_b_fc2, L1_cond_W_ada, L1_cond_b_ada, L2_cond_g1, L2_cond_g2, L2_cond_qkv_w, L2_cond_qkv_b, L2_cond_qg, L2_cond_kg, L2_cond_proj_w, L2_cond_proj_b, L2_cond_fc1_w, L2_cond_fc1_b, L2_cond_fc2_w, L2_cond_fc2_b, L2_cond_ada_w, L2_cond_ada_b, L3_cond_qkv_w, L3_cond_qkv_b, L3_cond_proj_w, L3_cond_proj_b, L3_cond_fc1_w, L3_cond_fc1_b, L3_cond_fc2_w, L3_cond_fc2_b, L3_cond_ada_w, L3_cond_ada_b):
    import jax
    import jax.numpy as jnp

    def _L0_cond_ref(x, c, w_adaln, b_adaln, w_qkv, b_qkv, w_proj, b_proj, w_gate, w1, b1, w2, b2):
        import jax, jax.numpy as jnp
        import numpy as np
        NUM_HEADS = 16
        NUM_EXPERTS = 4
        TOP_K = 2
        LN_EPS = 1e-06

        def _ln(h):
            mu = jnp.mean(h, axis=-1, keepdims=True)
            var = jnp.var(h, axis=-1, keepdims=True)
            return (h - mu) * jax.lax.rsqrt(var + LN_EPS)

        def _modulate(h, shift, scale):
            return h * (1.0 + scale[:, None, :]) + shift[:, None, :]
        B, N, C = x.shape
        nh = NUM_HEADS
        hd = C // nh
        mod = jax.nn.silu(c) @ w_adaln + b_adaln
        sh_msa, sc_msa, g_msa, sh_mlp, sc_mlp, g_mlp = jnp.split(mod, 6, axis=-1)
        h = _modulate(_ln(x), sh_msa, sc_msa)
        qkv = (h @ w_qkv + b_qkv).reshape(B, N, 3, nh, hd).transpose(2, 0, 3, 1, 4)
        q, k, v = (qkv[0], qkv[1], qkv[2])
        attn = jax.nn.softmax(jnp.einsum('bhqd,bhkd->bhqk', q, k) * hd ** (-0.5), axis=-1)
        o = jnp.einsum('bhqk,bhkd->bhqd', attn, v).transpose(0, 2, 1, 3).reshape(B, N, C)
        o = o @ w_proj + b_proj
        x = x + g_msa[:, None, :] * o
        xn = _modulate(_ln(x), sh_mlp, sc_mlp)
        xf = xn.reshape(-1, C)
        gate_logits = xf @ w_gate
        topk_logits, topk_idx = jax.lax.top_k(gate_logits, TOP_K)
        gates = jax.nn.softmax(topk_logits, axis=-1)
        cw = jnp.sum(jax.nn.one_hot(topk_idx, NUM_EXPERTS, dtype=xf.dtype) * gates[..., None], axis=1)
        hmid = jax.nn.gelu(jnp.einsum('tc,ech->eth', xf, w1) + b1[:, None, :], approximate=True)
        eo = jnp.einsum('eth,ehc->etc', hmid, w2) + b2[:, None, :]
        moe = jnp.einsum('te,etc->tc', cw, eo).reshape(B, N, C)
        return x + g_mlp[:, None, :] * moe

    def _L1_cond_ref(x, c, W_qkv, b_qkv, W_proj, b_proj, W_fc1, b_fc1, W_fc2, b_fc2, W_ada, b_ada):
        import jax, jax.numpy as jnp
        import numpy as np
        B, L, C = (8, 128, 144)
        H = 16
        D = C // H
        FF = int(C * 4.0)
        EPS = 1e-06

        def _layernorm(x):
            mu = jnp.mean(x, axis=-1, keepdims=True)
            var = jnp.mean(jnp.square(x - mu), axis=-1, keepdims=True)
            return (x - mu) * jax.lax.rsqrt(var + EPS)

        def _modulate(x, shift, scale):
            return x * (1.0 + scale) + shift

        def _attention(h, W_qkv, b_qkv, W_proj, b_proj):
            b, l, c = h.shape
            qkv = h @ W_qkv + b_qkv
            qkv = qkv.reshape(b, l, 3, H, D)
            q, k, v = (qkv[:, :, 0], qkv[:, :, 1], qkv[:, :, 2])
            scale = D ** (-0.5)
            scores = jnp.einsum('blhd,bmhd->bhlm', q * scale, k)
            attn = jax.nn.softmax(scores, axis=-1)
            o = jnp.einsum('bhlm,bmhd->blhd', attn, v).reshape(b, l, c)
            return o @ W_proj + b_proj
        ada = jax.nn.silu(c) @ W_ada + b_ada
        shift_msa, scale_msa, gate_msa, shift_mlp, scale_mlp, gate_mlp = jnp.split(ada, 6, axis=-1)
        h = _modulate(_layernorm(x), shift_msa, scale_msa)
        x = x + gate_msa * _attention(h, W_qkv, b_qkv, W_proj, b_proj)
        h = _modulate(_layernorm(x), shift_mlp, scale_mlp)
        mlp = jax.nn.gelu(h @ W_fc1 + b_fc1, approximate=True) @ W_fc2 + b_fc2
        x = x + gate_mlp * mlp
        return x

    def _L2_cond_ref(x, c, g1, g2, qkv_w, qkv_b, qg, kg, proj_w, proj_b, fc1_w, fc1_b, fc2_w, fc2_b, ada_w, ada_b):
        import jax, jax.numpy as jnp
        import numpy as np
        DIM = 144
        HEADS = 16
        HEAD_DIM = DIM // HEADS
        HIDDEN = int(DIM * 4.0)
        EPS = 1e-12

        def rmsnorm(x, g, d):
            n = jnp.linalg.norm(x, axis=-1, keepdims=True)
            return x / jnp.maximum(n, EPS) * d ** 0.5 * g

        def modulate(x, scale, shift):
            return x * (1.0 + scale[:, None, :]) + shift[:, None, :]
        B, N, D = x.shape
        mod = jax.nn.silu(c) @ ada_w.T + ada_b
        shift_msa, scale_msa, gate_msa, shift_mlp, scale_mlp, gate_mlp = jnp.split(mod, 6, axis=-1)
        gate_msa = jnp.tanh(gate_msa)
        gate_mlp = jnp.tanh(gate_mlp)
        h = modulate(rmsnorm(x, g1, D), scale_msa, shift_msa)
        qkv = h @ qkv_w.T + qkv_b
        qkv = qkv.reshape(B, N, 3, HEADS, HEAD_DIM).transpose(2, 0, 3, 1, 4)
        q, k, v = (qkv[0], qkv[1], qkv[2])
        q = rmsnorm(q, qg, HEAD_DIM)
        k = rmsnorm(k, kg, HEAD_DIM)
        q = q * HEAD_DIM ** (-0.5)
        attn = jax.nn.softmax(jnp.einsum('bhqd,bhkd->bhqk', q, k), axis=-1)
        o = jnp.einsum('bhqk,bhkd->bhqd', attn, v)
        o = o.transpose(0, 2, 1, 3).reshape(B, N, D)
        o = o @ proj_w.T + proj_b
        x = x + gate_msa[:, None, :] * o
        h2 = modulate(rmsnorm(x, g2, D), scale_mlp, shift_mlp)
        m = jax.nn.gelu(h2 @ fc1_w.T + fc1_b, approximate=True) @ fc2_w.T + fc2_b
        x = x + gate_mlp[:, None, :] * m
        return x

    def _L3_cond_ref(x, c, qkv_w, qkv_b, proj_w, proj_b, fc1_w, fc1_b, fc2_w, fc2_b, ada_w, ada_b):
        import jax, jax.numpy as jnp
        import numpy as np
        N, T, D, H = (32, 128, 144, 16)
        DH = D // H
        MLP = int(D * 4.0)
        EPS = 1e-06

        def _layernorm(x):
            m = jnp.mean(x, axis=-1, keepdims=True)
            v = jnp.var(x, axis=-1, keepdims=True)
            return (x - m) * jax.lax.rsqrt(v + EPS)

        def _modulate(x, shift, scale):
            return x * (1.0 + scale[:, None, :]) + shift[:, None, :]

        def _attention(x, qkv_w, qkv_b, proj_w, proj_b):
            n, t, d = x.shape
            scale = DH ** (-0.5)
            qkv = x @ qkv_w + qkv_b
            qkv = qkv.reshape(n, t, 3, H, DH)
            q, k, v = (qkv[:, :, 0], qkv[:, :, 1], qkv[:, :, 2])
            attn = jnp.einsum('nthd,ntkd->nthk', q * scale, k)
            attn = jax.nn.softmax(attn, axis=-1)
            out = jnp.einsum('nthk,ntkd->nthd', attn, v)
            out = out.transpose(0, 2, 1, 3).reshape(n, t, d)
            return out @ proj_w + proj_b

        def _mlp(x, fc1_w, fc1_b, fc2_w, fc2_b):
            h = jax.nn.gelu(x @ fc1_w + fc1_b, approximate=False)
            return h @ fc2_w + fc2_b
        ada = jax.nn.silu(c) @ ada_w + ada_b
        shift_msa, scale_msa, gate_msa, shift_mlp, scale_mlp, gate_mlp = jnp.split(ada, 6, axis=1)
        x = x + gate_msa[:, None, :] * _attention(_modulate(_layernorm(x), shift_msa, scale_msa), qkv_w, qkv_b, proj_w, proj_b)
        x = x + gate_mlp[:, None, :] * _mlp(_modulate(_layernorm(x), shift_mlp, scale_mlp), fc1_w, fc1_b, fc2_w, fc2_b)
        return x
    x = _L0_cond_ref(x, cond_1152, L0_cond_w_adaln, L0_cond_b_adaln, L0_cond_w_qkv, L0_cond_b_qkv, L0_cond_w_proj, L0_cond_b_proj, L0_cond_w_gate, L0_cond_w1, L0_cond_b1, L0_cond_w2, L0_cond_b2)
    x = _L1_cond_ref(x, cond_1152[:, None, :], L1_cond_W_qkv, L1_cond_b_qkv, L1_cond_W_proj, L1_cond_b_proj, L1_cond_W_fc1, L1_cond_b_fc1, L1_cond_W_fc2, L1_cond_b_fc2, L1_cond_W_ada, L1_cond_b_ada)
    x = _L2_cond_ref(x, cond_1152, L2_cond_g1, L2_cond_g2, L2_cond_qkv_w, L2_cond_qkv_b, L2_cond_qg, L2_cond_kg, L2_cond_proj_w, L2_cond_proj_b, L2_cond_fc1_w, L2_cond_fc1_b, L2_cond_fc2_w, L2_cond_fc2_b, L2_cond_ada_w, L2_cond_ada_b)
    x = _L3_cond_ref(x, cond_1152, L3_cond_qkv_w, L3_cond_qkv_b, L3_cond_proj_w, L3_cond_proj_b, L3_cond_fc1_w, L3_cond_fc1_b, L3_cond_fc2_w, L3_cond_fc2_b, L3_cond_ada_w, L3_cond_ada_b)
    return x

_drawn_inputs = setup_inputs


def setup_inputs(seed=0):
    import zlib

    import numpy as np

    out = dict(_drawn_inputs(seed))
    spreads = {'L0_cond_b_adaln': (0.0, 0.546),
     'L0_cond_b_qkv': (0.0, 0.8),
     'L0_cond_b_proj': (0.0, 0.457),
     'L0_cond_b1': (0.0, 0.8),
     'L0_cond_b2': (0.0, 0.685),
     'L1_cond_b_qkv': (0.0, 0.8),
     'L1_cond_b_proj': (0.0, 0.494),
     'L1_cond_b_fc1': (0.0, 0.8),
     'L1_cond_b_fc2': (0.0, 0.462),
     'L1_cond_b_ada': (0.0, 0.538),
     'L2_cond_qkv_b': (0.0, 0.8),
     'L2_cond_proj_b': (0.0, 0.479),
     'L2_cond_fc1_b': (0.0, 0.8),
     'L2_cond_fc2_b': (0.0, 0.523),
     'L2_cond_ada_b': (0.0, 0.55)}
    factors = {'L0_cond_w_adaln': 2.971,
     'L0_cond_w_qkv': 8.0,
     'L0_cond_w_proj': 8.0,
     'L0_cond_w_gate': 5.619,
     'L0_cond_w1': 7.274,
     'L0_cond_w2': 6.609,
     'L1_cond_W_qkv': 8.0,
     'L1_cond_W_proj': 8.0,
     'L1_cond_W_fc1': 5.326,
     'L1_cond_W_fc2': 4.877,
     'L2_cond_qkv_w': 8.0,
     'L2_cond_proj_w': 8.0,
     'L2_cond_fc1_w': 5.185,
     'L2_cond_fc2_w': 4.806,
     'L3_cond_qkv_w': 8.0,
     'L3_cond_qkv_b': 8.0,
     'L3_cond_proj_w': 8.0,
     'L3_cond_proj_b': 25.506,
     'L3_cond_fc1_w': 6.634,
     'L3_cond_fc1_b': 8.0,
     'L3_cond_fc2_w': 6.525,
     'L3_cond_fc2_b': 32.386,
     'L3_cond_ada_w': 5.739,
     'L3_cond_ada_b': 8.0}
    for name, (base, spread) in spreads.items():
        noise = np.random.default_rng([zlib.crc32(name.encode()), seed]).standard_normal(out[name].shape)
        drawn = base * np.exp(spread * noise) if base else spread * noise
        out[name] = jnp.asarray(drawn.astype(out[name].dtype))
    for name, factor in factors.items():
        out[name] = (out[name] * factor).astype(out[name].dtype)
    return out
```

```python
import math
from contextlib import ExitStack

import concourse.bass as bass
from concourse import mybir

F32 = mybir.dt.float32
F32R = mybir.dt.float32r
BF16 = mybir.dt.bfloat16
I32 = mybir.dt.int32
ALU = mybir.AluOpType
ACT = mybir.ActivationFunctionType
AX = mybir.AxisListType

B, T, C = 32, 128, 144
H, D = 16, 9
HID = 576
E = 4
L = 4
G = 4
NG = B // G
TG = G * T
CM = 128
CR_CH = C - CM
REM = 4 * CR_CH + 2
HEADS_TILE = 12
QK_ROWS = [108, 108, 72]
KS = 6 * D
TB = T // H
TOK_ROWS = [96, 96, 96]
TOK_V = [96, 48]
TOK_KS = KS + TB
MASK = -1e30
KT = HID // 128 + 1
TAIL = HID - 128 * (KT - 1)
VS = D + 1
VW = H * VS + 32
CR = 64
LN_EPS = 1e-6
RMS_EPS2 = 1e-24
MAGIC = 0x5F3759DF
FC1_OF = [E * KT, KT, KT, KT]
Y_OF = [E * 2, 2, 2, 2]
SH1, SC1, SH2, SC2 = range(4)


def build(nc, io):
    ctx = ExitStack()
    with ctx:
        def sb(name, shape, dt=F32):
            return ctx.enter_context(nc.sbuf_tensor(name, shape, dt))

        def sem(name):
            return ctx.enter_context(nc.semaphore(name))

        X = sb("X", [T, B, C])
        ident = sb("ident", [128, 128])
        maskf = sb("maskf", [TB, 2, T])
        maskb = sb("maskb", [TB, 2, T], BF16)
        identb = sb("identb", [128, 128], BF16)
        masks = sb("masks", [128, 2])
        gains = sb("gains", [128, 4])
        g12 = sb("g12", [128, 2])
        mhalf = sb("mhalf", [128, G])
        si = sb("si", [128, B])
        sir = sb("sir", [CR_CH + 1, B])
        wqkv = sb("wqkv", [CM, L, 3 * C])
        wproj = sb("wproj", [CM, L, C])
        wfc1 = sb("wfc1", [CM, L + E - 1, HID])
        wfc2 = sb("wfc2", [128, L + E - 1, KT, C])
        wgate = sb("wgate", [CM, E])
        rqkv = sb("rqkv", [REM, L, 3 * C], F32R)
        rproj = sb("rproj", [REM, L, C], F32R)
        rfc1 = sb("rfc1", [REM, L + E - 1, HID], F32R)
        rgate = sb("rgate", [REM - 2, E], F32R)
        wtmp = sb("wtmp", [REM, HID], F32R)
        modm = sb("modm", [CM, L, 4, B])
        modr = sb("modr", [REM - 2, L, 4, B])
        gbuf = sb("gbuf", [T, 2, G, C])
        stat = sb("stat", [T, G, 6])
        mv = sb("mv", [T, 2, G, 2])
        rstd = sb("rstd", [T, 2, G])
        xn = sb("xn", [T, 2, G, C])
        xr = sb("xr", [T, 2, G, 4, CR_CH])
        hT = sb("hT", [CM, 2, TG])
        hmod = sb("hmod", [REM - 2, TG])
        hhi = sb("hhi", [REM - 2, TG], F32R)
        hr = sb("hr", [REM, 2, TG], F32R)
        parts = sb("parts", [108, 3, 3, TG], BF16)
        res = sb("res", [108, 2, TG])
        qk = sb("qk", [128, 2, 2, 8, TG], BF16)
        negm = sb("negm", [T, 2, H], BF16)
        mT = sb("mT", [H, 2, T], BF16)
        prob = sb("prob", [T, 4, 512])
        V = sb("V", [T, 2, G, VW])
        OT = sb("OT", [128, 2, 512])
        rec = sb("rec", [T, 2, H])
        On = sb("On", [T, G, C])
        Onr = sb("Onr", [T, G, 4, CR_CH])
        OnT = sb("OnT", [CM, TG])
        ohi = sb("ohi", [REM - 2, TG], F32R)
        onr = sb("onr", [REM, TG], F32R)
        gx = sb("gx", [T, 2, 2, C])
        hid = sb("hid", [128, KT, TG])
        acc = On
        lg = sb("lg", [T, G, E])
        rank = sb("rank", [T, G, E])
        cmpb = sb("cmpb", [T, G, E])
        lmax = sb("lmax", [T, G])
        ebase = sb("ebase", [T, G, E])
        cw = sb("cw", [T, G, E])
        csum = sb("csum", [T, G])
        ss = sb("ss", [T, G, 2 * H])
        rs = sb("rs", [T, G, 2 * H])
        rt = sb("rt", [T, G, 2 * H])
        hid_f = hid[:].rearrange("p k t -> p (k t)")
        qs = hid_f[:, 0:G * 2 * C].rearrange("t (b n) -> t b n", b=G)
        sq = hid_f[:, G * 2 * C:(G + 2) * 2 * C].rearrange("t (b n) -> t b n", b=2)
        vt = wfc1[0:TOK_V[0], L - 1:L + 1, 0:TG]
        vT = hid_f[0:G * D, 0:H * T]
        gsb = parts[0:B].rearrange("p m a t -> p (m a t)").bitcast(F32)[:, 0:L * 2 * C].rearrange("b (l n) -> b l n", l=L)
        qk_f = qk[:].rearrange("p a b h t -> p (a b h t)").bitcast(F32)
        ada = qk_f[:, 0:L * 6 * C].rearrange("p (l n) -> p l n", l=L)
        adar = qk_f[0:CR_CH + 1, L * 6 * C:2 * L * 6 * C].rearrange("p (l n) -> p l n", l=L)
        ada4 = qk_f[:, 2 * L * 6 * C:2 * L * 6 * C + 2 * 2 * 4 * 4 * CR_CH] \
            .rearrange("p (a k n) -> p a k n", a=4, k=4)
        NST = 4
        stage = hid[:].rearrange("p k t -> p (k t)")[0:REM, 0:NST * HID].rearrange("p (s n) -> p s n", s=NST)

        bank = [ctx.enter_context(nc.psum_tensor(f"bank{i}", [128, 512], F32)) for i in range(8)]

        qk_scr = nc.dram_tensor("qk_scr", [2, 3, D, 2 * H, TG], BF16, kind="Internal").ap()
        tok_scr = nc.dram_tensor("tok_scr", [2, 2, G, 3, D, H, T], BF16, kind="Internal").ap()
        v_scr = nc.dram_tensor("v_scr", [2, G, D, H, T], F32, kind="Internal").ap()
        gate_scr = nc.dram_tensor("gate_scr", [L, 2, B, C], F32, kind="Internal").ap()

        q_c, q_x0, q_x1, q_w0 = sem("q_c"), sem("q_x0"), sem("q_x1"), sem("q_w0")
        q_ada = [sem(f"q_ada{l}") for l in range(L)]
        q_w1 = sem("q_w1")
        q_st = [sem(f"q_st{i}") for i in range(NST)]
        q_gs, q_out = sem("q_gs"), sem("q_out")
        q_w, q_r = sem("q_w"), sem("q_r")
        q_vw, q_vr, q_mask = sem("q_vw"), sem("q_vr"), sem("q_mask")
        q_m = [sem("q_m0"), sem("q_m1")]
        q_g = [sem("q_g0"), sem("q_g1")]
        s_ada, s_ht, s_hr, s_qk, s_qt = sem("s_ada"), sem("s_ht"), sem("s_hr"), sem("s_qk"), sem("s_qt")
        s_v, s_sm, s_mt, s_st, s_pv = sem("s_v"), sem("s_sm"), sem("s_mt"), sem("s_st"), sem("s_pv")
        s_ot, s_otok, s_ont, s_onr, s_pj = sem("s_ot"), sem("s_otok"), sem("s_ont"), sem("s_onr"), sem("s_pj")
        s_fc1, s_y, s_lg, s_vt = sem("s_fc1"), sem("s_y"), sem("s_lg"), sem("s_vt")
        a_si, a_gt, a_ht, a_p1, a_qt = sem("a_si"), sem("a_gt"), sem("a_ht"), sem("a_p1"), sem("a_qt")
        a_sq, a_exp, a_v, a_ot, a_ont = sem("a_sq"), sem("a_exp"), sem("a_v"), sem("a_ot"), sem("a_ont")
        a_gelu, a_vt = sem("a_gelu"), sem("a_vt")
        d_set, d_wa, d_ws, d_mod, d_stat = sem("d_set"), sem("d_wa"), sem("d_ws"), sem("d_mod"), sem("d_stat")
        d_mv, d_xn, d_hm, d_ha, d_hr = sem("d_mv"), sem("d_xn"), sem("d_hm"), sem("d_ha"), sem("d_hr")
        d_r1, d_p2, d_sm, d_mt, d_rec = sem("d_r1"), sem("d_p2"), sem("d_sm"), sem("d_mt"), sem("d_rec")
        d_on, d_oa, d_onr, d_gate, d_ss = sem("d_on"), sem("d_oa"), sem("d_onr"), sem("d_gate"), sem("d_ss")
        d_nw, d_qn, d_top, d_cw, d_y = sem("d_nw"), sem("d_qn"), sem("d_top"), sem("d_cw"), sem("d_y")
        d_rep, d_xr, d_ox = sem("d_rep"), sem("d_xr"), sem("d_ox")
        g_zero, g_set, g_ra, g_rb, g_rc = sem("g_zero"), sem("g_set"), sem("g_ra"), sem("g_rb"), sem("g_rc")
        g_rd, g_rs, g_p3, g_x, g_ew = sem("g_rd"), sem("g_rs"), sem("g_p3"), sem("g_x"), sem("g_ew")
        alone = sem("alone")

        block = ctx.enter_context(nc.Block())

        chunks = [("qkv", l) for l in range(1)] + [("proj", 0), ("gate", 0)] + [("fc1", L - 1 + e) for e in range(E)]
        for l in range(1, L):
            chunks += [("qkv", l), ("proj", l), ("fc1", l - 1)]
        NEAR = 2
        WIDTH = {"qkv": 3 * C, "proj": C, "fc1": HID, "gate": E}
        SPLIT = {"qkv": rqkv, "proj": rproj, "fc1": rfc1}

        def qk_tiles(l):
            return TOK_ROWS if l == 3 else QK_ROWS

        def written(l, n):
            return 144 * (n + 1) if l < 3 else 144 * 24 + 192 * (n + 1 - 24)

        def read(l, n):
            return 192 * (n + 1) if l < 3 else 192 * 24 + 288 * (n + 1 - 24)

        def fc1_slot(l, e):
            return L - 1 + e if l == 0 else l - 1

        fc1_base = [8 * sum(FC1_OF[:l]) for l in range(L + 1)]
        y_base = [8 * sum(Y_OF[:l]) for l in range(L + 1)]

        @block.sync
        def _(sp):
            def load_chunk(i):
                what, k = chunks[i]
                n = WIDTH[what]
                if i >= NST:
                    sp.wait_ge(d_ws, CR + i - NST + 1)
                src, bias = io.rest(what, k)
                sp.dma_start(stage[0:4 * CR_CH, i % NST, 0:n], src.unsqueeze(0).to_broadcast([4, CR_CH, n])) \
                    .then_inc(q_st[i % NST], 16)
                if bias is not None:
                    sp.dma_start(stage[4 * CR_CH:REM, i % NST, 0:n], bias.unsqueeze(0).to_broadcast([2, n])) \
                        .then_inc(q_st[i % NST], 16)

            sp.dma_start(si[:], io.cT[0:CM]).then_inc(q_c, 16)
            sp.wait_ge(d_set, CR + 1)
            sp.dma_start(sir[0:CR_CH], io.cT[CM:C]).then_inc(q_c, 16)
            sp.dma_start(ident[:], io.ident).then_inc(q_c, 16)
            sp.dma_start(masks[:], io.masks).then_inc(q_c, 16)
            sp.dma_start(maskf[:], io.block_mask).then_inc(q_c, 16)
            for i, a in enumerate(io.gains):
                sp.dma_start(gains[:, i:i + 1], a.unsqueeze(0).to_broadcast([128, 1])).then_inc(q_c, 16)
            sp.dma_start(ada[:, 0, :], io.ada_w[0][0:CM, :]).then_inc(q_ada[0], 16)
            sp.dma_start(adar[0:CR_CH, 0, :], io.ada_w[0][CM:C, :]).then_inc(q_ada[0], 16)
            sp.dma_start(adar[CR_CH:CR_CH + 1, 0, :], io.ada_b[0].unsqueeze(0)).then_inc(q_ada[0], 16)
            xv = io.x.rearrange("b t c -> t b c")
            sp.dma_start(X[:, 0:2 * G, :], xv[:, 0:2 * G, :]).then_inc(q_x0, 16)
            sp.dma_start(wqkv[:, 0, :], io.qkv_w[0][0:CM, :]).then_inc(q_w0, 16)
            sp.dma_start(wproj[:, 0, :], io.proj_w[0][0:CM, :]).then_inc(q_w0, 16)
            for i in range(NEAR):
                load_chunk(i)
            for l in range(1, L):
                sp.dma_start(ada[:, l, :], io.ada_w[l][0:CM, :]).then_inc(q_ada[l], 16)
                sp.dma_start(adar[0:CR_CH, l, :], io.ada_w[l][CM:C, :]).then_inc(q_ada[l], 16)
                sp.dma_start(adar[CR_CH:CR_CH + 1, l, :], io.ada_b[l].unsqueeze(0)).then_inc(q_ada[l], 16)
            sp.dma_start(X[:, 2 * G:B, :], xv[:, 2 * G:B, :]).then_inc(q_x1, 16)
            for l in range(L):
                sp.wait_ge(a_gt, CR + l + 1)
                sp.dma_start(gate_scr[l].rearrange("w b c -> b w c"), gsb[:, l, :].rearrange("b (w c) -> b w c", w=2)) \
                    .then_inc(q_gs, 16)
            for i in range(NEAR, NST + NEAR):
                load_chunk(i)

            def far_weights():
                for l in range(1, L):
                    sp.dma_start(wqkv[:, l, :], io.qkv_w[l][0:CM, :]).then_inc(q_w1, 16)
                    sp.dma_start(wproj[:, l, :], io.proj_w[l][0:CM, :]).then_inc(q_w1, 16)
                sp.dma_start(wgate[:], io.gate_w[0:CM, :]).then_inc(q_w1, 16)
                for k in range(L + E - 1):
                    w1, w2, b2 = io.mlp(k)
                    sp.dma_start(wfc1[:, k, :], w1[0:CM, :]).then_inc(q_w1, 16)
                    sp.dma_start(wfc2[:, k, 0:KT - 1, :], w2[0:128 * (KT - 1), :].rearrange("(k p) c -> p k c", p=128)) \
                        .then_inc(q_w1, 16)
                    sp.dma_start(wfc2[0:TAIL, k, KT - 1, :], w2[128 * (KT - 1):HID, :]).then_inc(q_w1, 16)
                    sp.dma_start(wfc2[TAIL:TAIL + 1, k, KT - 1, :], b2.unsqueeze(0)).then_inc(q_w1, 16)

            def load_gates(l, w, g, p, n1):
                sp.wait_ge(d_gate, CR + 2 * n1 - 2)
                sp.dma_start(gbuf[:, p, :, :].rearrange("t b c -> t (b c)"),
                             gate_scr[l, w, bass.ds(G * g, G), :].rearrange("b c -> (b c)").unsqueeze(0)
                             .to_broadcast([T, G * C])).then_inc(q_g[p], 16)

            def write_parts(l, n, p):
                for m in range(3):
                    nh = QK_ROWS[m] // D
                    sp.wait_ge(a_p1, CR + 3 * n + m + 1)
                    sp.wait_ge(d_p2, CR + 3 * n + m + 1)
                    sp.wait_ge(g_p3, CR + 3 * n + m + 1)
                    for part in range(3):
                        if l < 3:
                            sp.dma_start(qk_scr[p, part].rearrange("d h t -> h d t")[HEADS_TILE * m:HEADS_TILE * m + nh],
                                         parts[0:QK_ROWS[m], m, part, :]).then_inc(q_w, 16)
                            continue
                        d0, d1 = 6 * m, 6 * m + 6
                        for side in range(2):
                            a, b = max(d0, D * side), min(d1, D * side + D)
                            if a < b:
                                sp.dma_start(tok_scr[p, side, :, part, a - D * side:b - D * side]
                                             .rearrange("b d h t -> (d h) b t"),
                                             parts[H * (a - d0):H * (b - d0), m, part, :]
                                             .rearrange("r (b t) -> r b t", b=G)).then_inc(q_w, 16)
                if l == 3:
                    for m in range(2):
                        sp.wait_ge(a_vt, CR + 2 * (n - 24) + m + 1)
                        sp.dma_start(v_scr[p, :, 6 * m:6 * m + TOK_V[m] // H].rearrange("b d h t -> (d h) b t"),
                                     vt[0:TOK_V[m], m, :].rearrange("r (b t) -> r b t", b=G)).then_inc(q_vw, 16)

            def read_parts(l, n, p):
                sp.wait_ge(s_st, CR + 16 * (n - 1))
                sp.wait_ge(q_w, written(l, n))
                for s in range(2):
                    r0 = 64 * s
                    for part in range(3):
                        rows = (3 - part) * D
                        if l < 3:
                            hq, hk = slice(8 * s, 8 * s + 8), slice(H + 8 * s, H + 8 * s + 8)
                            src = qk_scr[p].rearrange("a d h t -> (a d) h t")
                            sp.dma_start(qk[r0:r0 + rows, p, 0, :, :], src[0:rows, hq, :]).then_inc(q_r, 16)
                            k_part = src[D * part:D * part + D, hk, :].rearrange("d h t -> d (h t)")
                            k_part = k_part.unsqueeze(0).to_broadcast([3 - part, D, 8 * TG])
                            sp.dma_start(qk[r0:r0 + rows, p, 1, :, :], k_part).then_inc(q_r, 16)
                        else:
                            bs = slice(2 * s, 2 * s + 2)
                            dst = qk[r0:r0 + rows, p].rearrange("r s h t -> r s (h t)") \
                                .rearrange("r s (b x) -> r s b x", b=2)
                            sp.dma_start(dst[:, 0], tok_scr[p, 0].rearrange("b a d h t -> (a d) b (h t)")[0:rows, bs]) \
                                .then_inc(q_r, 16)
                            for i in range(3 - part):
                                sp.dma_start(dst[D * i:D * i + D, 1],
                                             tok_scr[p, 1, :, part].rearrange("b d h t -> d b (h t)")[:, bs]) \
                                    .then_inc(q_r, 16)
                        r0 += rows
                if l == 3:
                    sp.wait_ge(s_v, CR + 2 * n)
                    sp.sem_inc(alone, 1)
                    sp.wait_ge(q_vw, 32 * (n + 1 - 24))
                    sp.dma_start(vT, v_scr[p].rearrange("b d h t -> (b d) (h t)")).then_inc(q_vr, 16)

            def write_max(l, u, up, b, p):
                if l < 3:
                    sp.wait_ge(d_mt, CR + u + 1)
                    sp.dma_start(qk[KS:KS + 65:64, p, 0, :, T * b:T * b + T], mT[:, up, :]).then_inc(q_m[up], 16)
                else:
                    sp.wait_ge(d_sm, CR + 4 * (u + 1))
                    r = 64 * (b // 2) + TOK_KS
                    row = qk[r:r + 1, p, 0].rearrange("r h t -> r (h t)")[:, H * T * (b % 2):H * T * (b % 2) + H * T]
                    sp.dma_start(row.rearrange("r (m t) -> r m t", t=H), negm[:, up, :]).then_inc(q_m[up], 16)

            def attention(l):
                n0, n1 = 8 * l, 16 * l
                if l == 0:
                    sp.wait_ge(q_gs, 16 * L)
                    sp.wait_ge(s_ada, CR + L)
                    sp.wait_ge(d_set, CR + 3)
                load_gates(l, 0, 0, 0, n1)
                if l == 3:
                    sp.wait_ge(s_st, CR + 16 * n0)
                    for p in range(2):
                        for side in range(2):
                            for r in (KS, 64 + KS):
                                sp.dma_start(qk[r:r + TB, p, side].rearrange("r h t -> r (h t)")
                                             .rearrange("r (x t) -> r x t", t=T),
                                             maskb[:, side, :].unsqueeze(1).to_broadcast([TB, 2 * H, T])) \
                                    .then_inc(q_mask, 16)
                write_parts(l, n0, 0)
                read_parts(l, n0, 0)
                write_parts(l, n0 + 1, 1)
                write_max(l, 4 * n0, 0, 0, 0)
                write_max(l, 4 * n0 + 1, 1, 1, 0)
                def step(g, p, f1, nxt):
                    n = n0 + g
                    if nxt:
                        read_parts(l, n + 1, 1 - p)
                        load_gates(l, 0, g + 1, 1 - p, n1 + g + 1)
                    for j in range(G):
                        u = 4 * n + j + 2
                        if j < 2:
                            write_max(l, u, j % 2, j + 2, p)
                        elif nxt:
                            write_max(l, u, j % 2, j - 2, 1 - p)
                    if f1:
                        write_parts(l, n + 2, p)

                with sp.Fori(0, 3) as i:
                    step(2 * i, 0, True, True)
                    step(2 * i + 1, 1, True, True)
                step(6, 0, False, True)
                step(7, 1, False, False)

            def mlp(l):
                n1 = 16 * l + 8
                load_gates(l, 1, 0, 0, n1)

                def step(g, p):
                    if l == L - 1:
                        sp.wait_ge(g_x, CR + 2 * (n1 + g + 1))
                        sp.dma_start(io.out.rearrange("b t c -> t b c")[:, bass.ds(G * g, G), :],
                                     X[:, bass.ds(G * g, G), :]).then_inc(q_out, 16)

                with sp.Fori(0, 3) as i:
                    load_gates(l, 1, 2 * i + 1, 1, n1 + 2 * i + 1)
                    step(2 * i, 0)
                    load_gates(l, 1, 2 * i + 2, 0, n1 + 2 * i + 2)
                    step(2 * i + 1, 1)
                load_gates(l, 1, 7, 1, n1 + 7)
                step(6, 0)
                step(7, 1)

            far_weights()
            for l in range(L):
                attention(l)
                if l == 0:
                    for i in range(NST + NEAR, len(chunks)):
                        load_chunk(i)
                mlp(l)
            sp.wait_ge(q_out, 16 * NG)

        @block.tensor
        def _(pe):
            for x in (s_ada, s_ht, s_hr, s_qk, s_qt, s_v, s_sm, s_mt, s_st, s_pv, s_ot, s_otok, s_ont, s_onr,
                      s_pj, s_fc1, s_y, s_lg, s_vt):
                pe.sem_inc(x, CR)

            def layer_mods(l):
                pe.wait_ge(q_ada[l], 48)
                pe.wait_ge(d_rep, CR + l + 1)
                if l >= 2:
                    pe.wait_ge(d_mod, CR + l - 1)
                    pe.wait_ge(a_gt, CR + l - 1)
                o = 3 * (l % 2)
                for k, col in enumerate((0, C, 3 * C, 4 * C)):
                    pe.matmul(bank[o][:, B * k:B * k + B], ada[:, l, col:col + CM], si[:], start=True, stop=False)
                    pe.matmul(bank[o][:, B * k:B * k + B], adar[:, l, col:col + CM], sir[:], start=False, stop=True)
                for k in range(4):
                    out = bank[o + 1][0:REM - 2, B * k:B * k + B]
                    pe.matmul(out, ada4[:, 2 * (l % 2), k, :], si[:], start=True, stop=False)
                    pe.matmul(out, ada4[0:CR_CH + 1, 2 * (l % 2) + 1, k, :], sir[:], start=False, stop=True)
                for k, col in enumerate((2 * C, 5 * C)):
                    pe.matmul(bank[o + 2][0:B, C * k:C * k + C], si[:], ada[:, l, col:col + C], start=True, stop=False)
                    mm = pe.matmul(bank[o + 2][0:B, C * k:C * k + C], sir[:], adar[:, l, col:col + C],
                                   start=False, stop=True)
                mm.then_inc(s_ada, 1)

            def t_main(n1, p, o):
                pe.wait_ge(d_xn, CR + 4 * (n1 + 1))
                for b in range(G):
                    mm = pe.transpose(bank[o][:, T * b:T * b + T], xn[:, p, b, 0:CM], ident[:])
                mm.then_inc(s_ht, 1)

            def t_rem(n1, p, o):
                pe.wait_ge(d_xr, CR + n1 + 1)
                pe.sem_inc(alone, 1)
                for b in range(G):
                    mm = pe.transpose(bank[o][0:REM - 2, T * b:T * b + T],
                                      xr[:, p, b].rearrange("t r c -> t (r c)"), ident[:])
                mm.then_inc(s_hr, 1)

            def q_and_k(l, n, n1, p):
                pe.wait_ge(a_ht, CR + 4 * (n1 + 1))
                pe.wait_ge(d_hr, CR + n1 + 1)
                if l == 2:
                    for b, o in enumerate((0, 1, 3, 4)):
                        pe.matmul(bank[o][:, 0:2 * C], hT[:, p, T * b:T * b + T], wqkv[:, l, 0:2 * C],
                                  start=True, stop=False)
                        pe.matmul(bank[o][:, 0:2 * C], hr[:, p, T * b:T * b + T], rqkv[:, l, 0:2 * C],
                                  start=False, stop=True).then_inc(s_qt, 1)
                    pe.wait_ge(a_qt, CR + 4 * (n - 16 + 1))
                    pe.wait_ge(d_qn, CR + 8 * (n - 16 + 1))
                    for m in range(3):
                        for b in range(G):
                            mm = pe.transpose(bank[m][0:QK_ROWS[m], T * b:T * b + T],
                                              qs[:, b, 108 * m:108 * m + QK_ROWS[m]], ident[:])
                        mm.then_inc(s_qk, 1)
                    return
                for m, rows in enumerate(qk_tiles(l)):
                    cols = slice(qk_tiles(l)[0] * m, qk_tiles(l)[0] * m + rows)
                    out = bank[m][0:rows, :]
                    pe.matmul(out, wqkv[:, l, cols], hT[:, p, :], start=True, stop=False)
                    pe.matmul(out, rqkv[:, l, cols], hr[:, p, :], start=False, stop=True).then_inc(s_qk, 1)

            def values_t(p):
                for m, rows in enumerate(TOK_V):
                    cols = slice(2 * C + TOK_V[0] * m, 2 * C + TOK_V[0] * m + rows)
                    out = bank[3 + m][0:rows, :]
                    pe.matmul(out, wqkv[:, 3, cols], hT[:, p, :], start=True, stop=False)
                    pe.matmul(out, rqkv[:, 3, cols], hr[:, p, :], start=False, stop=True).then_inc(s_vt, 1)

            def values(l, p, q):
                if l == 3:
                    for i in range(H // 2):
                        mm = pe.transpose(bank[3 + q][:, G * D * i:G * D * i + G * D],
                                          vT[:, H // 2 * q + i:H * T:H], ident[0:G * D, 0:G * D])
                    mm.then_inc(s_v, 1)
                    return
                for b in (2 * q, 2 * q + 1):
                    out = bank[3 + q][:, C * (b % 2):C * (b % 2) + C]
                    pe.matmul(out, hT[:, p, T * b:T * b + T], wqkv[:, l, 2 * C:3 * C], start=True, stop=False)
                    mm = pe.matmul(out, hr[:, p, T * b:T * b + T], rqkv[:, l, 2 * C:3 * C], start=False, stop=True)
                mm.then_inc(s_v, 1)

            def operand(l, side, p, b, h, with_max):
                if l < 3:
                    s = h // 8
                    return qk[64 * s:64 * s + KS + with_max, p, side, h % 8, T * b:T * b + T]
                s, at = b // 2, H * T * (b % 2)
                return qk[64 * s:64 * s + TOK_KS + with_max, p, side].rearrange("r h t -> r (h t)")[:, at + h:at + H * T:H]

            def scores_for_max(l, u, b, p, c):
                pe.wait_ge(d_sm, CR + 4 * u + c - 1)
                for i in range(4):
                    h = 4 * c + i
                    mm = pe.matmul(bank[3 + c % 2][:, T * i:T * i + T], operand(l, 0, p, b, h, 0),
                                   operand(l, 1, p, b, h, 0), start=True, stop=True)
                mm.then_inc(s_sm, 1)

            def turn_max(u, up):
                pe.wait_ge(d_sm, CR + 4 * (u + 1))
                pe.wait_ge(d_mt, CR + u)
                pe.transpose(bank[5][:].bitcast(BF16)[0:H, 0:T], negm[:, up, :], identb[:]).then_inc(s_mt, 1)

            def scores(l, K, b, p, c):
                for i in range(4):
                    h = 4 * c + i
                    mm = pe.matmul(bank[c % 2][:, T * i:T * i + T], operand(l, 1, p, b, h, 1),
                                   operand(l, 0, p, b, h, 1), start=True, stop=True)
                mm.then_inc(s_st, 1)

            def weigh(K, nb, b, p, c):
                pe.wait_ge(a_exp, CR + K + 1)
                if c == 0:
                    pe.wait_ge(a_ot, CR + nb)
                    if b == 0:
                        pe.wait_ge(d_onr, CR + weigh.n)
                for i in range(4):
                    h = 4 * c + i
                    mm = pe.matmul(bank[6][32 * i:32 * i + 32, T * c:T * c + T], V[:, p, b, VS * h:VS * h + 32],
                                   prob[:, c, T * i:T * i + T], start=True, stop=True)
                mm.then_inc(s_pv, 1)

            def to_tokens(nb, par):
                pe.wait_ge(a_ot, CR + nb + 1)
                pe.wait_ge(d_on, CR + nb)
                for c in range(4):
                    mm = pe.transpose(bank[7][:, T * c:T * c + T], OT[:, par, T * c:T * c + T], ident[:])
                mm.then_inc(s_otok, 1)

            def project(l, n, n1):
                pe.wait_ge(d_on, CR + 4 * (n + 1))
                for b in range(G):
                    mm = pe.transpose(bank[7][:, T * b:T * b + T], On[:, b, 0:CM], ident[:])
                mm.then_inc(s_ont, 1)
                pe.wait_ge(d_ox, CR + n + 1)
                pe.sem_inc(alone, 1)
                for b in range(G):
                    mm = pe.transpose(bank[6][0:REM - 2, T * b:T * b + T],
                                      Onr[:, b].rearrange("t r c -> t (r c)"), ident[:])
                mm.then_inc(s_onr, 1)
                pe.wait_ge(a_ont, CR + n + 1)
                pe.wait_ge(d_onr, CR + n + 1)
                for q in range(2):
                    for b in (2 * q, 2 * q + 1):
                        out = bank[5 + 2 * q][:, C * (b % 2):C * (b % 2) + C]
                        pe.matmul(out, OnT[:, T * b:T * b + T], wproj[:, l, :], start=True, stop=False)
                        mm = pe.matmul(out, onr[:, T * b:T * b + T], rproj[:, l, :], start=False, stop=True)
                    mm.then_inc(s_pj, 1)

            def attention(l):
                n0, m0 = 8 * l, 16 * l
                if l == 0:
                    pe.wait_ge(q_w0, 32)
                    pe.wait_ge(d_ws, CR + NEAR)
                    pe.wait_ge(d_mod, CR + L)
                    pe.wait_ge(a_gt, CR + L)
                    pe.wait_ge(g_set, CR + 1)
                    pe.wait_ge(d_set, CR + 2)
                else:
                    pe.wait_ge(a_gelu, CR + fc1_base[l])
                    pe.wait_ge(d_gate, CR + 2 * m0)
                for g in range(2):
                    if g == 1:
                        pe.wait_ge(d_r1, CR + 3 * n0 + 3)
                        if l == 2:
                            pe.wait_ge(a_v, CR + 2 * (n0 + 1))
                    t_main(m0 + g, g, 2)
                    t_rem(m0 + g, g, 5)
                    q_and_k(l, n0 + g, m0 + g, g)
                    if l == 3:
                        pe.wait_ge(a_vt, CR + 2 * g)
                        values_t(g)
                    elif g == 0:
                        if l == 2:
                            pe.wait_ge(a_qt, CR + 4)
                        values(l, 0, 0)
                        values(l, 0, 1)
                if l == 3:
                    pe.wait_ge(a_vt, CR + 4)
                    pe.wait_ge(q_vr, 16)
                    values(l, 0, 0)
                    values(l, 0, 1)
                    pe.wait_ge(q_mask, 16 * 8)
                pe.wait_ge(a_v, CR + 2 * (n0 + 1))
                pe.wait_ge(d_hm, CR + 4 * (m0 + 2))
                if l == 2:
                    pe.wait_ge(a_qt, CR + 8)
                pe.wait_ge(q_r, read(l, n0))
                for j in range(3):
                    for c in range(4):
                        scores_for_max(l, 4 * n0 + j, j, 0, c)
                    if j < 2 and l < 3:
                        turn_max(4 * n0 + j, j)

                def step(g, p, f1, nxt):
                    n, n1 = n0 + g, m0 + g
                    weigh.n = n
                    for j in range(G):
                        nb = 4 * n + j
                        if j == 0:
                            pe.wait_ge(d_gate, CR + 2 * n1)
                        if l < 3 and (j < 2 or nxt):
                            turn_max(nb + 2, j % 2)
                        if j == 1 and nxt:
                            pe.wait_ge(q_r, read(l, n + 1))
                        if j == 2 and f1:
                            pe.wait_ge(d_r1, CR + 3 * (n + 2))
                            t_main(n1 + 2, p, 2)
                        if j == 3 and f1:
                            if l < 3:
                                pe.wait_ge(d_mt, CR + nb + 3)
                            t_rem(n1 + 2, p, 5)
                        for c in range(4):
                            K = 4 * nb + c
                            if c == 0:
                                pe.wait_ge(q_m[j % 2], 16 * (2 * n + j // 2 + 1))
                            if j == 0 and c < 2 and nxt:
                                pe.wait_ge(d_r1, CR + 3 * (n + 1) + c + 1)
                            else:
                                pe.wait_ge(a_exp, CR + K - 1)
                            scores(l, K, j, p, c)
                            if j > 0 or c >= 2:
                                kk = 4 * j + c - 2
                                weigh(K - 2, 4 * n + kk // 4, kk // 4, p, kk % 4)
                            if j == 0:
                                scores_for_max(l, nb + 3, 3, p, c)
                            elif nxt:
                                scores_for_max(l, nb + 3, j - 1, 1 - p, c)
                            if c == 3 and j > 0:
                                to_tokens(nb - 1, (j - 1) % 2)
                    for c in (2, 3):
                        weigh(16 * n + 12 + c, 4 * n + 3, 3, p, c)
                    if f1:
                        pe.wait_ge(a_exp, CR + 16 * (n + 1))
                        if l == 2:
                            pe.wait_ge(d_sm, CR + 4 * (4 * n + 7))
                        q_and_k(l, n + 2, n1 + 2, p)
                    if nxt:
                        pe.wait_ge(d_sm, CR + 4 * (4 * n + 7))
                        if l == 3:
                            if f1:
                                values_t(p)
                                pe.wait_ge(a_vt, CR + 2 * (n - 24 + 3))
                                pe.sem_inc(alone, 1)
                            pe.wait_ge(q_vr, 16 * (n - 24 + 2))
                            pe.sem_inc(alone, 1)
                        if l == 2 and f1:
                            pe.wait_ge(a_qt, CR + 4 * (n - 16 + 3))
                        values(l, 1 - p, 0)
                        values(l, 1 - p, 1)
                    to_tokens(4 * n + 3, 1)
                    if f1:
                        pe.wait_ge(d_hm, CR + 4 * (n1 + 3))
                    if l < 3:
                        pe.wait_ge(d_mt, CR + (4 * n + (6 if nxt else 4)))
                    project(l, n, n1)
                    if nxt:
                        pe.wait_ge(a_v, CR + 2 * (n + 2))

                with pe.Fori(0, 3) as i:
                    step(2 * i, 0, True, True)
                    step(2 * i + 1, 1, True, True)
                step(6, 0, False, True)
                step(7, 1, False, False)

            def mlp(l):
                m0 = 16 * l + 8
                n_last = 8 * (l + 1)
                if l == 0:
                    pe.wait_ge(q_w1, 16 * (2 * (L - 1) + 1 + 4 * (L + E - 1)))
                    pe.wait_ge(d_ws, CR + len(chunks) + 1)
                pe.wait_ge(a_exp, CR + 16 * n_last)
                pe.wait_ge(d_gate, CR + 2 * m0)
                pe.wait_ge(d_onr, CR + n_last)

                def first(e, f0):
                    for m in range(KT):
                        rows = min(128, HID - 128 * m)
                        cols = slice(128 * m, 128 * m + rows)
                        k = fc1_slot(l, e)
                        out = bank[2 + m % 3][0:rows, :]
                        if m < 3:
                            pe.wait_ge(a_gelu, CR + f0)
                        else:
                            pe.wait_ge(a_gelu, CR + f0 + m - 2)
                        pe.matmul(out, wfc1[:, k, cols], hT[:, first.p, :], start=True, stop=False)
                        pe.matmul(out, rfc1[:, k, cols], hr[:, first.p, :], start=False, stop=True) \
                            .then_inc(s_fc1, 1)

                def second(e, f0, y0, n1):
                    k = fc1_slot(l, e)
                    for q in range(2):
                        if l == 0:
                            pe.wait_ge(d_y, CR + y0 + q - 1)
                        else:
                            pe.wait_ge(d_gate, CR + 2 * n1 + q - 1)
                        for b in (2 * q, 2 * q + 1):
                            out = bank[5 + q][:, C * (b % 2):C * (b % 2) + C]
                            for t in range(KT):
                                if q == 0 and b == 0:
                                    pe.wait_ge(a_gelu, CR + f0 + t + 1)
                                rows = 128 if t < KT - 1 else TAIL + 1
                                mm = pe.matmul(out, hid[0:rows, t, T * b:T * b + T], wfc2[0:rows, k, t, :],
                                               start=(t == 0), stop=(t == KT - 1))
                        mm.then_inc(s_y, 1)

                def gate_logits(p):
                    for b in range(G):
                        out = bank[7][:, E * b:E * b + E]
                        pe.matmul(out, hT[:, p, T * b:T * b + T], wgate[:], start=True, stop=False)
                        mm = pe.matmul(out, hr[0:REM - 2, p, T * b:T * b + T], rgate[:], start=False, stop=True)
                    mm.then_inc(s_lg, 1)

                def step(g, p, nxt):
                    n1 = m0 + g
                    first.p = p
                    pe.wait_ge(a_ht, CR + 4 * (n1 + 1))
                    pe.wait_ge(d_hr, CR + n1 + 1)
                    if l == 0:
                        pe.wait_ge(d_top, CR + 2 * g)
                        gate_logits(p)
                    for e in range(E if l == 0 else 1):
                        f0 = fc1_base[l] + FC1_OF[l] * g + KT * e
                        first(e, f0)
                        if e == 0 and nxt:
                            t_main(n1 + 1, 1 - p, 0)
                            t_rem(n1 + 1, 1 - p, 1)
                        second(e, f0, y_base[l] + Y_OF[l] * g + 2 * e, n1)

                t_main(m0, 0, 0)
                t_rem(m0, 0, 1)
                with pe.Fori(0, 3) as i:
                    step(2 * i, 0, True)
                    step(2 * i + 1, 1, True)
                step(6, 0, True)
                step(7, 1, False)

            pe.wait_ge(q_c, 16 * 9)
            pe.wait_ge(a_si, CR + 2)
            for l in range(L):
                layer_mods(l)
            for l in range(L):
                attention(l)
                mlp(l)

        @block.scalar
        def _(act):
            for x in (a_si, a_gt, a_ht, a_p1, a_qt, a_sq, a_exp, a_v, a_ot, a_ont, a_gelu, a_vt):
                act.sem_inc(x, CR)

            def mod_main(l, which, g, p, n1, o):
                act.wait_ge(s_ht, CR + n1 + 1)
                for b in range(G):
                    at = bass.ds(G * g + b, 1)
                    act.activation(hT[:, p, T * b:T * b + T], bank[o][:, T * b:T * b + T], ACT.Identity,
                                   scale=modm[:, l, 2 * which + 1, at], bias=modm[:, l, 2 * which, at]) \
                        .then_inc(a_ht, 1)

            def part1(l, n, q_reuse):
                for m, rows in enumerate(qk_tiles(l)):
                    act.wait_ge(s_qk, CR + 3 * n + m + 1)
                    if m == 0 and q_reuse:
                        act.wait_ge(q_w, written(l, n - 1))
                    act.activation(parts[0:rows, m, 0, :], bank[m][0:rows, :], ACT.Copy).then_inc(a_p1, 1)

            def values_t_out(n, q_reuse):
                for m, rows in enumerate(TOK_V):
                    act.wait_ge(s_vt, CR + 2 * (n - 24) + m + 1)
                    if m == 0 and q_reuse:
                        act.wait_ge(q_vw, 32 * (n - 24))
                    act.activation(vt[0:rows, m, :], bank[3 + m][0:rows, :], ACT.Copy).then_inc(a_vt, 1)

            def head_squares(n):
                for b, o in enumerate((0, 1, 3, 4)):
                    r = 4 * (n - 16) + b
                    act.wait_ge(s_qt, CR + r + 1)
                    act.wait_ge(d_ss, CR + r - 1)
                    act.activation(sq[:, b % 2, :], bank[o][:, 0:2 * C], ACT.Square).then_inc(a_sq, 1)
                    act.activation(qs[:, b, :], bank[o][:, 0:2 * C], ACT.Copy).then_inc(a_qt, 1)

            def values_out(l, n, p, q):
                act.wait_ge(s_v, CR + 2 * n + q + 1)
                if l == 3:
                    out = V[:, p, :, VS * H // 2 * q:VS * H // 2 * (q + 1)].rearrange("t b (h e) -> t b h e", e=VS)
                    act.activation(out[:, :, :, 0:D], bank[3 + q][:, 0:2 * C].rearrange("t (h b d) -> t b h d", b=G, d=D),
                                   ACT.Copy).then_inc(a_v, 1)
                    return
                out = V[:, p, 2 * q:2 * q + 2, 0:H * VS].rearrange("t b (h e) -> t b h e", e=VS)[:, :, :, 0:D]
                act.activation(out, bank[3 + q][:, 0:2 * C].rearrange("t (b h d) -> t b h d", b=2, h=H), ACT.Copy) \
                    .then_inc(a_v, 1)

            def attention(l):
                n0, m0 = 8 * l, 16 * l
                scale = 3.0 if l == 2 else float(D) ** -0.5
                for g in range(2):
                    mod_main(l, 0, g, g, m0 + g, 2)
                    if l == 2:
                        head_squares(n0 + g)
                    part1(l, n0 + g, n0 + g > 0)
                    if l == 3:
                        values_t_out(n0 + g, g > 0)
                    if g == (l == 3):
                        values_out(l, n0, 0, 0)
                        values_out(l, n0, 0, 1)

                def out_of_bank6(nb, par):
                    act.wait_ge(s_pv, CR + 4 * (nb + 1))
                    act.wait_ge(s_otok, CR + nb - 1)
                    act.activation(OT[:, par, :], bank[6][:], ACT.Copy).then_inc(a_ot, 1)

                def step(g, p, f1, nxt):
                    n, n1 = n0 + g, m0 + g
                    for j in range(G):
                        nb = 4 * n + j
                        for c in range(4):
                            K = 4 * nb + c
                            act.wait_ge(s_st, CR + K + 1)
                            act.wait_ge(s_pv, CR + K - 3)
                            act.activation(prob[:, c, :], bank[c % 2][:], ACT.Exp, scale=scale) \
                                .then_inc(a_exp, 1)
                            if j == 2 and c == 3 and f1:
                                mod_main(l, 0, g + 2, p, n1 + 2, 2)
                            if j > 0 and c == 2:
                                out_of_bank6(nb - 1, (j - 1) % 2)
                    out_of_bank6(4 * n + 3, 1)
                    if f1:
                        if l == 2:
                            head_squares(n + 2)
                        part1(l, n + 2, True)
                        if l == 3:
                            values_t_out(n + 2, True)
                    if nxt:
                        values_out(l, n + 1, 1 - p, 0)
                        values_out(l, n + 1, 1 - p, 1)
                    act.wait_ge(s_ont, CR + n + 1)
                    act.activation(OnT[:], bank[7][:], ACT.Copy).then_inc(a_ont, 1)

                with act.Fori(0, 3) as i:
                    step(2 * i, 0, True, True)
                    step(2 * i + 1, 1, True, True)
                step(6, 0, False, True)
                step(7, 1, False, False)

            def mlp(l):
                m0 = 16 * l + 8
                func = ACT.Gelu if l == 3 else ACT.Gelu_apprx_tanh
                mod_main(l, 1, 0, 0, m0, 0)
                if l == 0:
                    act.wait_ge(d_ws, CR + len(chunks) + 1)

                def step(g, p, nxt):
                    for e in range(E if l == 0 else 1):
                        f0 = fc1_base[l] + FC1_OF[l] * g + KT * e
                        y0 = y_base[l] + Y_OF[l] * g + 2 * e
                        for m in range(KT):
                            rows = min(128, HID - 128 * m)
                            act.wait_ge(s_fc1, CR + f0 + m + 1)
                            if m == 0:
                                act.wait_ge(s_y, CR + y0)
                            act.activation(hid[0:rows, m, :], bank[2 + m % 3][0:rows, :], func) \
                                .then_inc(a_gelu, 1)
                        if e == 0 and nxt:
                            mod_main(l, 1, g + 1, 1 - p, m0 + g + 1, 0)

                with act.Fori(0, 3) as i:
                    step(2 * i, 0, True)
                    step(2 * i + 1, 1, True)
                step(6, 0, True)
                step(7, 1, False)

            act.wait_ge(q_c, 16 * 9)
            act.activation(si[:], si[:], ACT.Silu).then_inc(a_si, 1)
            act.activation(sir[0:CR_CH], sir[0:CR_CH], ACT.Silu).then_inc(a_si, 1)
            for l in range(L):
                act.wait_ge(s_ada, CR + l + 1)
                act.activation(gsb[:, l, :], bank[3 * (l % 2) + 2][0:B, 0:2 * C], ACT.Tanh if l == 2 else ACT.Copy) \
                    .then_inc(a_gt, 1)
            act.wait_ge(d_mod, CR + L)
            act.wait_ge(q_gs, 16 * L)
            for l in range(L):
                attention(l)
                mlp(l)

        @block.vector
        def _(dve):
            for x in (d_set, d_wa, d_ws, d_mod, d_stat, d_mv, d_xn, d_hm, d_ha, d_hr, d_r1, d_p2, d_sm, d_mt,
                      d_rec, d_on, d_oa, d_onr, d_gate, d_ss, d_nw, d_qn, d_top, d_cw, d_y, d_rep, d_xr,
                      d_ox):
                dve.sem_inc(x, CR)
            def split_chunk(i):
                what, k = chunks[i]
                n = WIDTH[what]
                rows = REM - 2 if what == "gate" else REM
                dve.wait_ge(q_st[i % NST], sum((16 if chunks[x][0] == "gate" else 32) for x in range(i % NST, i + 1, NST)))
                st = stage[0:rows, i % NST, 0:n]
                out = rgate[:] if what == "gate" else SPLIT[what][:, k, :]
                dve.wait_ge(d_ws, CR + i)
                dve.tensor_copy(wtmp[0:rows, 0:n], st).then_inc(d_wa, 1)
                dve.wait_ge(d_wa, CR + i + 1)
                dve.scalar_tensor_tensor(out, wtmp[0:rows, 0:n].bitcast(F32), masks[0:rows, 1:2], st,
                                         ALU.mult, ALU.add).then_inc(d_ws, 1)

            def stats(l, which, g, p, n1):
                if not (l == 0 and which == 0):
                    dve.wait_ge(g_x, CR + 2 * (n1 - 7))
                dve.wait_ge(d_mv, CR + 4 * n1)
                for b in range(G):
                    dve.bn_stats(stat[:, b, :], X[:, bass.ds(G * g + b, 1), :].rearrange("t b c -> t (b c)")) \
                        .then_inc(d_stat, 1)
                dve.wait_ge(g_rs, CR + n1 - 1)
                for b in range(G):
                    dve.wait_ge(d_stat, CR + 4 * n1 + b + 1)
                    dve.sem_inc(alone, 1)
                    dve.bn_aggr(mv[:, p, b, :], stat[:, b, :]).then_inc(d_mv, 1)

            def normalise(l, g, p, n1):
                dve.wait_ge(g_rs, CR + n1 + 1)
                dve.wait_ge(s_hr, CR + n1 - 1)
                for b in range(G):
                    x = X[:, bass.ds(G * g + b, 1), :].rearrange("t b c -> t (b c)")
                    if l == 2:
                        dve.tensor_scalar(xn[:, p, b, :], x, rstd[:, p, b:b + 1], None, ALU.mult) \
                            .then_inc(d_xn, 1)
                    else:
                        dve.tensor_scalar(xn[:, p, b, :], x, mv[:, p, b, 0:1], rstd[:, p, b:b + 1],
                                          ALU.subtract, ALU.mult).then_inc(d_xn, 1)
                dve.wait_ge(d_xn, CR + 4 * (n1 + 1))
                dve.tensor_copy(xr[:, p], xn[:, p, :, CM:C].unsqueeze(2).to_broadcast([T, G, 4, CR_CH])) \
                    .then_inc(d_xr, 1)

            def mod_rem(l, which, g, p, n1, o):
                dve.wait_ge(s_hr, CR + n1 + 1)
                dve.wait_ge(d_hr, CR + n1)
                for b in range(G):
                    at = bass.ds(G * g + b, 1)
                    dve.tensor_scalar(hmod[:, T * b:T * b + T], bank[o][0:REM - 2, T * b:T * b + T],
                                      modr[:, l, 2 * which + 1, at], modr[:, l, 2 * which, at], ALU.mult, ALU.add) \
                        .then_inc(d_hm, 1)
                dve.wait_ge(d_hm, CR + 4 * (n1 + 1))
                dve.tensor_copy(hhi[:], hmod[:]).then_inc(d_ha, 1)
                dve.wait_ge(d_ha, CR + n1 + 1)
                dve.scalar_tensor_tensor(hr[0:REM - 2, p, :], hhi[:].bitcast(F32), masks[0:REM - 2, 0:1], hmod[:],
                                         ALU.mult, ALU.add).then_inc(d_hr, 1)

            def parts23(l, n):
                for m, rows in enumerate(qk_tiles(l)):
                    r = slice(0, rows)
                    i = 3 * n + m
                    dve.wait_ge(a_p1, CR + i + 1)
                    dve.wait_ge(g_p3, CR + (i - 1 if m else i))
                    dve.tensor_tensor(res[r, m % 2, :], bank[m][r, :], parts[r, m, 0, :], ALU.subtract) \
                        .then_inc(d_r1, 1)
                    dve.wait_ge(d_r1, CR + i + 1)
                    dve.tensor_copy(parts[r, m, 1, :], res[r, m % 2, :]).then_inc(d_p2, 1)

            def head_norms(n):
                r = n - 16
                for b in range(G):
                    dve.wait_ge(a_sq, CR + 4 * r + b + 1)
                    dve.tensor_reduce(ss[:, b, :], sq[:, b % 2, :].rearrange("t (h d) -> t h d", d=D), AX.X, ALU.add) \
                        .then_inc(d_ss, 1)
                k0 = 15 * r
                cnt = [0]

                def link(ins):
                    cnt[0] += 1
                    ins.then_inc(d_nw, 1)
                    dve.wait_ge(d_nw, CR + k0 + cnt[0])

                dve.wait_ge(d_ss, CR + 4 * (r + 1))
                s, y, t = (a[:].rearrange("t b h -> t (b h)") for a in (ss, rs, rt))
                link(dve.tensor_scalar(s, s, RMS_EPS2, None, ALU.max))
                link(dve.tensor_scalar(t.bitcast(I32), s.bitcast(I32), 1, None, ALU.arith_shift_right))
                link(dve.tensor_scalar(y.bitcast(I32), t.bitcast(I32), -1.0, float(MAGIC), ALU.mult, ALU.add))
                for _ in range(3):
                    link(dve.tensor_tensor(t, y, y, ALU.mult))
                    link(dve.tensor_tensor(t, t, s, ALU.mult))
                    link(dve.tensor_scalar(t, t, -0.5, 1.5, ALU.mult, ALU.add))
                    link(dve.tensor_tensor(y, y, t, ALU.mult))
                assert cnt[0] == 15
                dve.wait_ge(a_qt, CR + 4 * (r + 1))
                for b in range(G):
                    for w in range(2):
                        v = qs[:, b, C * w:C * w + C].rearrange("t (h d) -> t h d", d=D)
                        dve.scalar_tensor_tensor(v, v, gains[:, 2 + w:3 + w],
                                                 rs[:, b, H * w:H * w + H].unsqueeze(2).to_broadcast([T, H, D]),
                                                 ALU.mult, ALU.mult).then_inc(d_qn, 1)

            def head_max(l, u, up, c):
                dve.wait_ge(s_sm, CR + 4 * u + c + 1)
                if l < 3:
                    dve.wait_ge(s_mt, CR + u - 1)
                elif c == 0:
                    dve.wait_ge(q_m[up], head_max.count)
                dve.tensor_reduce(negm[:, up, 4 * c:4 * c + 4], bank[3 + c % 2][:].rearrange("q (h k) -> q h k", k=T),
                                  AX.X, ALU.max, negate=True).then_inc(d_sm, 1)

            def max_out(u, up):
                dve.wait_ge(s_mt, CR + u + 1)
                if not isinstance(u, int) or u >= 2:
                    dve.wait_ge(q_m[up], max_out.count)
                dve.tensor_copy(mT[:, up, :], bank[5][:].bitcast(BF16)[0:H, 0:T]).then_inc(d_mt, 1)

            def attention(l):
                n0, m0 = 8 * l, 16 * l

                def normed(nb, b):
                    dve.wait_ge(s_otok, CR + nb + 1)
                    o = bank[7][:].rearrange("q (h e) -> q h e", e=32)
                    if b == 0:
                        dve.wait_ge(s_onr, CR + normed.n)
                    dve.reciprocal(rec[:, b % 2, :], o[:, :, D]).then_inc(d_rec, 1)
                    dve.wait_ge(d_rec, CR + nb + 1)
                    dve.tensor_tensor(On[:, b, :].rearrange("q (h d) -> q h d", d=D), o[:, :, 0:D],
                                      rec[:, b % 2, :].unsqueeze(2).to_broadcast([T, H, D]), ALU.mult) \
                        .then_inc(d_on, 1)

                def add_back(n, n1, p):
                    dve.wait_ge(q_g[p], add_back.count)
                    for q in range(2):
                        dve.wait_ge(s_pj, CR + 2 * n + q + 1)
                        dve.wait_ge(g_x, CR + 2 * n1 + q - 1)
                        dve.tensor_tensor(gx[:, q, :, :], bank[5 + 2 * q][:, 0:2 * C].rearrange("t (b c) -> t b c", b=2),
                                          gbuf[:, p, 2 * q:2 * q + 2, :], ALU.mult).then_inc(d_gate, 1)

                for g in range(2):
                    stats(l, 0, g, g, m0 + g)
                for g in range(2):
                    normalise(l, g, g, m0 + g)
                for g in range(2):
                    mod_rem(l, 0, g, g, m0 + g, 5)
                    if l == 2:
                        head_norms(n0 + g)
                    parts23(l, n0 + g)
                if l == 0:
                    dve.wait_ge(q_x1, 16)
                for j in range(3):
                    for c in range(4):
                        head_max.count = 16 * (2 * n0 + j // 2)
                        head_max(l, 4 * n0 + j, j % 2, c)
                    if j < 2 and l < 3:
                        max_out.count = 16 * (2 * n0 + j // 2)
                        max_out(4 * n0 + j, j % 2)

                def step(g, p, f1, nxt):
                    n, n1 = n0 + g, m0 + g
                    normed.n = n
                    add_back.count = 16 * (8 * l + (g - p) // 2 + 1) if isinstance(g, int) else 16 * (8 * l + step.i + 1)
                    for j in range(G):
                        nb = 4 * n + j
                        head_max.count = 16 * (2 * n + (j + 1) // 2 + 1)
                        if l < 3 and (j < 2 or nxt):
                            max_out.count = 16 * (2 * n + (j + 2) // 2)
                            max_out(nb + 2, j % 2)
                        for c in range(4):
                            if j == 0 or nxt:
                                head_max(l, nb + 3, (j + 3) % 2, c)
                            if j == 0 and c == 1 and f1:
                                stats(l, 0, g + 2, p, n1 + 2)
                        if j == 1 and f1:
                            normalise(l, g + 2, p, n1 + 2)
                        if j > 0:
                            normed(nb - 1, j - 1)
                    if f1:
                        mod_rem(l, 0, g + 2, p, n1 + 2, 5)
                        if l == 2:
                            head_norms(n + 2)
                        parts23(l, n + 2)
                    normed(4 * n + 3, 3)
                    dve.wait_ge(d_on, CR + 4 * (n + 1))
                    dve.tensor_copy(Onr[:], On[:, :, CM:C].unsqueeze(2).to_broadcast([T, G, 4, CR_CH])) \
                        .then_inc(d_ox, 1)
                    dve.wait_ge(s_onr, CR + n + 1)
                    dve.wait_ge(s_pj, CR + 2 * n)
                    dve.tensor_copy(ohi[:], bank[6][0:REM - 2, :]).then_inc(d_oa, 1)
                    dve.wait_ge(d_oa, CR + n + 1)
                    dve.scalar_tensor_tensor(onr[0:REM - 2, :], ohi[:].bitcast(F32), masks[0:REM - 2, 0:1],
                                             bank[6][0:REM - 2, :], ALU.mult, ALU.add).then_inc(d_onr, 1)
                    add_back(n, n1, p)

                with dve.Fori(0, 3) as i:
                    step.i = i
                    step(2 * i, 0, True, True)
                    step(2 * i + 1, 1, True, True)
                step(6, 0, False, True)
                step(7, 1, False, False)

            def top2(g, p):
                dve.wait_ge(s_lg, CR + g + 1)
                lv = bank[7][:, 0:G * E].rearrange("t (b e) -> t b e", e=E)
                k0 = 16 * g
                cnt = [0]

                def link(ins):
                    cnt[0] += 1
                    ins.then_inc(d_cw, 1)
                    dve.wait_ge(d_cw, CR + k0 + cnt[0])

                dve.wait_ge(d_y, CR + y_base[0] + Y_OF[0] * g)
                dve.wait_ge(g_ew, CR + g)
                dve.tensor_copy(lg[:], lv).then_inc(d_top, 1)
                dve.wait_ge(d_top, CR + 2 * g + 1)
                link(dve.tensor_reduce(lmax[:], lg[:], AX.X, ALU.max))
                for e in range(E):
                    ins = dve.memset(rank[:, :, e], float(E - 1 - e))
                link(ins)
                for d in range(1, E):
                    lo, hi = slice(0, E - d), slice(d, E)
                    link(dve.tensor_tensor(cmpb[:, :, lo], lg[:, :, lo], lg[:, :, hi], ALU.is_ge))
                    link(dve.tensor_tensor(rank[:, :, lo], rank[:, :, lo], cmpb[:, :, lo], ALU.subtract))
                    link(dve.tensor_tensor(rank[:, :, hi], rank[:, :, hi], cmpb[:, :, lo], ALU.add))
                dve.tensor_tensor(lg[:], lg[:], lmax[:].unsqueeze(2).to_broadcast([T, G, E]), ALU.subtract) \
                    .then_inc(d_top, 1)
                link(dve.tensor_scalar(rank[:], rank[:], 2.0, None, ALU.is_lt))
                dve.wait_ge(g_ew, CR + g + 1)
                link(dve.tensor_tensor(cw[:], cw[:], rank[:], ALU.mult))
                link(dve.tensor_reduce(csum[:], cw[:], AX.X, ALU.add))
                link(dve.reciprocal(csum[:], csum[:]))
                link(dve.tensor_tensor(cw[:], cw[:], csum[:].unsqueeze(2).to_broadcast([T, G, E]), ALU.mult))
                assert cnt[0] == 16

            def mlp(l):
                m0 = 16 * l + 8

                def gated(src, q, n1, p):
                    dve.wait_ge(g_x, CR + 2 * n1 + q - 1)
                    dve.tensor_tensor(gx[:, q, :, :], src, gbuf[:, p, 2 * q:2 * q + 2, :], ALU.mult) \
                        .then_inc(d_gate, 1)

                def step(g, p, nxt, gates):
                    n1 = m0 + g
                    if nxt:
                        stats(l, 1, g + 1, 1 - p, n1 + 1)
                        normalise(l, g + 1, 1 - p, n1 + 1)
                    if l == 0:
                        top2(g, p)
                    if nxt:
                        mod_rem(l, 1, g + 1, 1 - p, n1 + 1, 1)
                    y0 = y_base[l] + Y_OF[l] * g
                    if l == 0:
                        dve.wait_ge(d_gate, CR + 2 * n1)
                        for e in range(E):
                            for q in range(2):
                                dve.wait_ge(s_y, CR + y0 + 2 * e + q + 1)
                                if e:
                                    dve.wait_ge(d_y, CR + y0 + 2 * e + q - 1)
                                for b in (2 * q, 2 * q + 1):
                                    y = bank[5 + q][:, C * (b % 2):C * (b % 2) + C]
                                    w = cw[:, b, e:e + 1]
                                    if e == 0:
                                        ins = dve.tensor_scalar(acc[:, b, :], y, w, None, ALU.mult)
                                    else:
                                        ins = dve.scalar_tensor_tensor(acc[:, b, :], y, w, acc[:, b, :],
                                                                       ALU.mult, ALU.add)
                                ins.then_inc(d_y, 1)
                        dve.wait_ge(q_g[p], gates)
                        dve.wait_ge(d_y, CR + y0 + 2 * E)
                        for q in range(2):
                            gated(acc[:, 2 * q:2 * q + 2, :], q, n1, p)
                    else:
                        dve.wait_ge(q_g[p], gates)
                        for q in range(2):
                            dve.wait_ge(s_y, CR + y0 + q + 1)
                            gated(bank[5 + q][:, 0:2 * C].rearrange("t (b c) -> t b c", b=2), q, n1, p)

                stats(l, 1, 0, 0, m0)
                normalise(l, 0, 0, m0)
                mod_rem(l, 1, 0, 0, m0, 1)
                with dve.Fori(0, 3) as i:
                    for p in range(2):
                        step(2 * i + p, p, True, 16 * (8 * l + 4 + i + 1))
                step(6, 0, True, 16 * (8 * l + 8))
                step(7, 1, False, 16 * (8 * l + 8))

            def replicate(l):
                dve.wait_ge(q_ada[l], 48)
                dve.wait_ge(s_ada, CR + l - 1)
                for a, src in ((0, ada[:, l, :]), (1, adar[:, l, :])):
                    rows = src.shape[0]
                    src = src.rearrange("p (w s c) -> p w s c", w=2, s=3)
                    for w in range(2):
                        out = ada4[0:rows, 2 * (l % 2) + a, 2 * w:2 * w + 2, :].rearrange("p s (r c) -> p s r c", r=4)
                        ins = dve.tensor_copy(out, src[:, w, 0:2, CM:C].unsqueeze(2).to_broadcast([rows, 2, 4, CR_CH]))
                ins.then_inc(d_rep, 1)

            def take_mods(l):
                o = 3 * (l % 2)
                dve.wait_ge(s_ada, CR + l + 1)
                for out, src in ((modm[:, l], bank[o][:, 0:4 * B]), (modr[:, l], bank[o + 1][0:REM - 2, 0:4 * B])):
                    out = out.rearrange("c (w s) b -> c w s b", s=2)
                    src = src.rearrange("c (w s b) -> c w s b", s=2, b=B)
                    dve.tensor_copy(out[:, :, 0, :], src[:, :, 0, :])
                    ins = dve.tensor_scalar(out[:, :, 1, :], src[:, :, 1, :], 1.0, None, ALU.add)
                ins.then_inc(d_mod, 1)

            dve.memset(sir[:], 1.0).then_inc(d_set, 1)
            dve.memset(mhalf[:], -0.5)
            dve.memset(hr[REM - 2:REM].bitcast(F32), 1.0)
            dve.memset(onr[REM - 2:REM].bitcast(F32), 1.0)
            dve.wait_ge(q_c, 16 * 9)
            dve.tensor_copy(identb[:], ident[:])
            dve.tensor_copy(maskb[:], maskf[:])
            dve.tensor_scalar(g12[:], gains[:, 0:2], float(C) ** 0.5, None, ALU.mult).then_inc(d_set, 1)
            replicate(0)
            for i in range(NEAR):
                split_chunk(i)
            for l in range(L):
                if l + 1 < L:
                    replicate(l + 1)
                take_mods(l)
            for r0 in (32, 96):
                ins = dve.memset(qk[r0:r0 + 32, :, 1, :, :], 1.0)
            ins.then_inc(d_set, 1)
            dve.wait_ge(d_mod, CR + L)
            dve.wait_ge(q_x0, 16)
            attention(0)
            for i in range(NEAR, len(chunks)):
                split_chunk(i)
            dve.wait_ge(d_ws, CR + len(chunks))
            dve.memset(hid[TAIL:TAIL + 1, KT - 1, :], 1.0).then_inc(d_ws, 1)
            mlp(0)
            for l in range(1, L):
                attention(l)
                mlp(l)

        @block.gpsimd
        def _(pool):
            for x in (g_zero, g_set, g_ra, g_rb, g_rc, g_rd, g_rs, g_p3, g_x, g_ew):
                pool.sem_inc(x, CR)

            def norm_factor(l, which, p, n1):
                pool.wait_ge(d_mv, CR + 4 * (n1 + 1))
                pool.wait_ge(d_xn, CR + 4 * (n1 - 1))
                pool.sem_inc(alone, 1)
                r = rstd[:, p, :]
                if l != 2:
                    pool.tensor_scalar(r, mv[:, p, :, 1], LN_EPS, None, ALU.add).then_inc(g_ra, 1)
                    pool.wait_ge(g_ra, CR + n1 + 1)
                    pool.tensor_tensor(r, r, mhalf[:], ALU.pow).then_inc(g_rs, 1)
                    return
                k = n1 - 32
                pool.tensor_tensor(r, mv[:, p, :, 0], mv[:, p, :, 0], ALU.mult).then_inc(g_ra, 1)
                pool.wait_ge(g_ra, CR + n1 + 1)
                pool.tensor_tensor(r, r, mv[:, p, :, 1], ALU.add).then_inc(g_rb, 1)
                pool.wait_ge(g_rb, CR + k + 1)
                pool.sem_inc(alone, 1)
                pool.tensor_scalar(r, r, float(C), RMS_EPS2, ALU.mult, ALU.max).then_inc(g_rc, 1)
                pool.wait_ge(g_rc, CR + k + 1)
                pool.tensor_tensor(r, r, mhalf[:], ALU.pow).then_inc(g_rd, 1)
                pool.wait_ge(g_rd, CR + k + 1)
                pool.sem_inc(alone, 1)
                pool.tensor_scalar(r, r, g12[:, which:which + 1], None, ALU.mult).then_inc(g_rs, 1)

            def part3(l, n):
                for m, rows in enumerate(qk_tiles(l)):
                    r = slice(0, rows)
                    pool.wait_ge(d_p2, CR + 3 * n + m + 1)
                    pool.tensor_tensor(parts[r, m, 2, :], res[r, m % 2, :], parts[r, m, 1, :], ALU.subtract) \
                        .then_inc(g_p3, 1)

            def add_to_x(g, n1):
                for q in range(2):
                    pool.wait_ge(d_gate, CR + 2 * n1 + q + 1)
                    x = X[:, bass.ds(G * g + 2 * q, 2), :]
                    pool.tensor_tensor(x, x, gx[:, q, :, :], ALU.add).then_inc(g_x, 1)

            def attention(l):
                n0, m0 = 8 * l, 16 * l

                def step(g, p, f1):
                    if f1:
                        norm_factor(l, 0, p, m0 + g + 2)
                        part3(l, n0 + g + 2)
                    add_to_x(g, m0 + g)

                for g in range(2):
                    norm_factor(l, 0, g, m0 + g)
                for g in range(2):
                    part3(l, n0 + g)
                with pool.Fori(0, 3) as i:
                    step(2 * i, 0, True)
                    step(2 * i + 1, 1, True)
                step(6, 0, False)
                step(7, 1, False)

            def mlp(l):
                m0 = 16 * l + 8

                def step(g, p, nxt):
                    if nxt:
                        norm_factor(l, 1, 1 - p, m0 + g + 1)
                    if l == 0:
                        pool.wait_ge(d_top, CR + 2 * g + 2)
                        pool.tensor_tensor(cw[:], ebase[:], lg[:], ALU.pow).then_inc(g_ew, 1)
                    add_to_x(g, m0 + g)

                norm_factor(l, 1, 0, m0)
                with pool.Fori(0, 3) as i:
                    step(2 * i, 0, True)
                    step(2 * i + 1, 1, True)
                step(6, 0, True)
                step(7, 1, False)

            pool.memset(V[:], 0.0).then_inc(g_zero, 1)
            pool.memset(ebase[:], math.e)
            pool.wait_ge(g_zero, CR + 1)
            ones = V[:].rearrange("t p b v -> t (p b) v")[:, :, 0:H * VS].rearrange("t a (h e) -> t a h e", e=VS)
            pool.memset(ones[:, :, :, D], 1.0).then_inc(g_set, 1)
            pool.wait_ge(d_set, CR + 2)
            for l in range(L):
                attention(l)
                mlp(l)


class Inputs:
    pass


def kernel(**inputs):
    import numpy as np
    import concourse.bacc as bacc
    from concourse.bass_utils import run_bass_kernel_spmd

    nc = bacc.Bacc("TRN2", target_bir_lowering=False, num_devices=1)
    arrays = {}

    def put(name, a):
        a = np.ascontiguousarray(a)
        arrays["in_" + name] = a
        return nc.dram_tensor("in_" + name, list(a.shape), F32, kind="ExternalInput").ap()

    def given(name, turned=False):
        a = np.asarray(inputs[name])
        return put(name, a.T if turned else a)

    io = Inputs()
    io.x = given("x")
    io.cT = given("cond_1152", turned=True)
    io.ident = put("ident", np.eye(128, dtype=np.float32))
    masks = np.zeros((128, 2), np.float32)
    masks[CR_CH:2 * CR_CH, 0] = masks[3 * CR_CH:4 * CR_CH, 0] = -1.0
    masks[2 * CR_CH:4 * CR_CH, 1] = masks[REM - 1, 1] = -1.0
    io.masks = put("masks", masks)
    own = np.arange(T)[None, :] // H == np.arange(TB)[:, None]
    io.block_mask = put("block_mask", np.stack([np.where(own, 0.0, MASK), own], axis=1).astype(np.float32))
    io.gains = [given("L2_cond_" + x) for x in ("g1", "g2", "qg", "kg")]
    ada = [("L0_cond_w_adaln", "L0_cond_b_adaln"), ("L1_cond_W_ada", "L1_cond_b_ada"),
           ("L2_cond_ada_w", "L2_cond_ada_b"), ("L3_cond_ada_w", "L3_cond_ada_b")]
    qkv = [("L0_cond_w_qkv", "L0_cond_b_qkv"), ("L1_cond_W_qkv", "L1_cond_b_qkv"),
           ("L2_cond_qkv_w", "L2_cond_qkv_b"), ("L3_cond_qkv_w", "L3_cond_qkv_b")]
    proj = [("L0_cond_w_proj", "L0_cond_b_proj"), ("L1_cond_W_proj", "L1_cond_b_proj"),
            ("L2_cond_proj_w", "L2_cond_proj_b"), ("L3_cond_proj_w", "L3_cond_proj_b")]
    fc1 = [("L1_cond_W_fc1", "L1_cond_b_fc1"), ("L2_cond_fc1_w", "L2_cond_fc1_b"), ("L3_cond_fc1_w", "L3_cond_fc1_b")]
    fc2 = [("L1_cond_W_fc2", "L1_cond_b_fc2"), ("L2_cond_fc2_w", "L2_cond_fc2_b"), ("L3_cond_fc2_w", "L3_cond_fc2_b")]

    def by_dim(a):
        return np.asarray(a).reshape(-1, 3, H, D).swapaxes(2, 3).reshape(np.shape(a))

    def pairs(names, turned):
        out = []
        for i, (w, b) in enumerate(names):
            if w == "L3_cond_qkv_w":
                out.append((put(w, by_dim(inputs[w])), put(b, by_dim(inputs[b]))))
            else:
                out.append((given(w, turned=(i == turned)), given(b)))
        return out

    ada, qkv, proj = pairs(ada, 2), pairs(qkv, 2), pairs(proj, 2)
    fc1, fc2 = pairs(fc1, 1), pairs(fc2, 1)
    w1, b1, w2, b2 = (given("L0_cond_" + x) for x in ("w1", "b1", "w2", "b2"))
    for e in range(E):
        fc1.append((w1[e], b1[e]))
        fc2.append((w2[e], b2[e]))
    io.ada_w, io.ada_b = [w for w, _ in ada], [b for _, b in ada]
    io.qkv_w, io.proj_w = [w for w, _ in qkv], [w for w, _ in proj]
    io.gate_w = given("L0_cond_w_gate")

    def rest(what, k):
        if what == "gate":
            return io.gate_w[CM:C, :], None
        w, b = {"qkv": qkv, "proj": proj, "fc1": fc1}[what][k]
        return w[CM:C, :], b

    io.rest = rest
    io.mlp = lambda k: (fc1[k][0], fc2[k][0], fc2[k][1])
    io.out = nc.dram_tensor("out", [B, T, C], F32, kind="ExternalOutput").ap()
    build(nc, io)
    result = run_bass_kernel_spmd(nc, [arrays], core_ids=[0])
    return result.results[0]["out"]
```

```python
import math
from contextlib import ExitStack

import concourse.bass as bass
from concourse import mybir

F32 = mybir.dt.float32
F32R = mybir.dt.float32r
BF16 = mybir.dt.bfloat16
I32 = mybir.dt.int32
ALU = mybir.AluOpType
ACT = mybir.ActivationFunctionType
AX = mybir.AxisListType

B, T, C = 32, 128, 144
H, D = 16, 9
HID = 576
E = 4
L = 4
G = 4
NG = B // G
TG = G * T
CM = 128
CR_CH = C - CM
REM = 4 * CR_CH + 2
QK_ROWS = 96
QK_DIMS = QK_ROWS // H
KS = 6 * D
TB = T // H
TOK_V = [96, 48]
MASK = -1e30
KT = HID // 128 + 1
TAIL = HID - 128 * (KT - 1)
VS = D + 1
VW = H * VS + 32
BF16_ONES = 1.0 + 0x3F80 / 2 ** 23
CR = 64
LN_EPS = 1e-6
RMS_EPS2 = 1e-24
MAGIC = 0x5F3759DF
FC1_OF = [E * KT, KT, KT, KT]
Y_OF = [E * 2, 2, 2, 2]
SH1, SC1, SH2, SC2 = range(4)
BY_TOKEN, BY_TOKEN_END = [(1, 1), (1, 2), (1, 3), (2, 0)], [(1, 2), (1, 3), (2, 0), (2, 1)]
TURNED, TURNED_END = [(3, 1), (3, 3)], [(3, 2), (3, 3)]
FACTORS, NORMS = {(2, 1): [0], (2, 2): [1], (2, 3): [2, 3]}, {(3, 0): [0], (3, 1): [1]}


def build(nc, io):
    ctx = ExitStack()
    with ctx:
        def sb(name, shape, dt=F32):
            return ctx.enter_context(nc.sbuf_tensor(name, shape, dt))

        def sem(name):
            return ctx.enter_context(nc.semaphore(name))

        X = sb("X", [T, B, C])
        ident = sb("ident", [128, 128])
        maskf = sb("maskf", [TB, 2, T])
        maskb = sb("maskb", [TB, 2, T], BF16)
        identb = sb("identb", [128, 128], BF16)
        masks = sb("masks", [128, 2])
        gains = sb("gains", [128, 4])
        g12 = sb("g12", [128, 2])
        mhalf = sb("mhalf", [128, G])
        si = sb("si", [128, B])
        sir = sb("sir", [CR_CH + 1, B])
        wqkv = sb("wqkv", [CM, L, 3 * C])
        wproj = sb("wproj", [CM, L, C])
        wfc1 = sb("wfc1", [CM, E, HID])
        wfc2 = sb("wfc2", [128, E, KT, C])
        wgate = sb("wgate", [CM, E])
        rqkv = sb("rqkv", [REM, L, 3 * C], F32R)
        rproj = sb("rproj", [REM, L, C], F32R)
        rfc1 = sb("rfc1", [REM, E, HID], F32R)
        rgate = sb("rgate", [REM - 2, E], F32R)
        wtmp = sb("wtmp", [REM, HID], F32R)
        modm = sb("modm", [CM, L, 4, B])
        modr = sb("modr", [REM - 2, L, 4, B])
        gbuf = sb("gbuf", [T, 2, G, C])
        stat = sb("stat", [T, G, 6])
        mv = sb("mv", [T, 2, G, 2])
        rstd = sb("rstd", [T, 2, G])
        xn = sb("xn", [T, 2, G, C])
        xr = sb("xr", [T, 2, G, 4, CR_CH])
        hT = sb("hT", [CM, 2, TG])
        hmod = sb("hmod", [REM - 2, TG])
        hhi = sb("hhi", [REM - 2, TG], F32R)
        hr = sb("hr", [REM, 2, TG], F32R)
        parts = sb("parts", [QK_ROWS, 3, 3, TG], BF16)
        res = sb("res", [QK_ROWS, 2, TG])
        qq = sb("qq", [128, 2, 2, 8, TG], BF16)
        kk = sb("kk", [128, 2, 8, TG], BF16)
        negm = sb("negm", [T, 2, H], BF16)
        mT = sb("mT", [H, 2, T], BF16)
        prob = sb("prob", [T, 4, 512])
        V = sb("V", [T, 2, G, VW])
        OT = sb("OT", [128, 2, 512])
        rec = sb("rec", [T, 2, H])
        On = sb("On", [T, G, C])
        Onr = sb("Onr", [T, G, 4, CR_CH])
        OnT = sb("OnT", [CM, TG])
        ohi = sb("ohi", [REM - 2, TG], F32R)
        onr = sb("onr", [REM, TG], F32R)
        gx = sb("gx", [T, 2, 2, C])
        hid = sb("hid", [128, KT, TG])
        acc = On
        lg = sb("lg", [T, G, E])
        rank = sb("rank", [T, G, E])
        cmpb = sb("cmpb", [T, G, E])
        lmax = sb("lmax", [T, G])
        ebase = sb("ebase", [T, G, E])
        cw = sb("cw", [T, G, E])
        csum = sb("csum", [T, G])
        ss = sb("ss", [T, G, 2 * H])
        rs = sb("rs", [T, G, 2 * H])
        rt = sb("rt", [T, G, 2 * H])
        hid_f = hid[:].rearrange("p k t -> p (k t)")
        qs = hid_f[:, 0:G * 2 * C].rearrange("t (b n) -> t b n", b=G)
        sq = hid_f[:, G * 2 * C:(G + 2) * 2 * C].rearrange("t (b n) -> t b n", b=2)
        vt = [wfc1[0:TOK_V[0], E - 1, 0:TG], wfc2[0:TOK_V[1], E - 1].rearrange("p k c -> p (k c)")[:, 0:TG]]
        vT = hid_f[0:G * D, 0:H * T]
        gsb = parts[0:B].rearrange("p m a t -> p (m a t)").bitcast(F32)[:, 0:L * 2 * C].rearrange("b (l n) -> b l n", l=L)
        qk_f = qq[:].rearrange("p a b h t -> p (a b h t)").bitcast(F32)
        ada = qk_f[:, 0:L * 6 * C].rearrange("p (l n) -> p l n", l=L)
        adar = qk_f[0:CR_CH + 1, L * 6 * C:2 * L * 6 * C].rearrange("p (l n) -> p l n", l=L)
        ada4 = qk_f[:, 2 * L * 6 * C:2 * L * 6 * C + 2 * 2 * 4 * 4 * CR_CH] \
            .rearrange("p (a k n) -> p a k n", a=4, k=4)
        NST = 4
        stage = hid[:].rearrange("p k t -> p (k t)")[0:REM, 0:NST * HID].rearrange("p (s n) -> p s n", s=NST)

        bank = [ctx.enter_context(nc.psum_tensor(f"bank{i}", [128, 512], F32)) for i in range(8)]

        qk_scr = nc.dram_tensor("qk_scr", [2, 2, 3, D, H, TG], BF16, kind="Internal").ap()
        tok_scr = nc.dram_tensor("tok_scr", [2, 2, G, 3, D, H, T], BF16, kind="Internal").ap()
        v_scr = nc.dram_tensor("v_scr", [2, G, D, H, T], F32, kind="Internal").ap()
        gate_scr = nc.dram_tensor("gate_scr", [L, 2, B, C], F32, kind="Internal").ap()

        q_c, q_x0, q_x1, q_w0 = sem("q_c"), sem("q_x0"), sem("q_x1"), sem("q_w0")
        q_ada = [sem(f"q_ada{l}") for l in range(L)]
        q_w1 = sem("q_w1")
        q_st = [sem(f"q_st{i}") for i in range(NST)]
        q_late, q_w2 = [sem(f"q_late{i}") for i in range(L - 1)], sem("q_w2")
        q_gs, q_out = sem("q_gs"), sem("q_out")
        q_w = sem("q_w")
        q_r = [[sem(f"q_r{p}{s}") for s in range(2)] for p in range(2)]
        q_vw, q_vr, q_mask = sem("q_vw"), sem("q_vr"), sem("q_mask")
        q_m = [sem("q_m0"), sem("q_m1")]
        q_g = [sem("q_g0"), sem("q_g1")]
        s_ada, s_ht, s_hr, s_qk, s_qt = sem("s_ada"), sem("s_ht"), sem("s_hr"), sem("s_qk"), sem("s_qt")
        s_v, s_sm, s_mt, s_st, s_pv = sem("s_v"), sem("s_sm"), sem("s_mt"), sem("s_st"), sem("s_pv")
        s_ot, s_otok, s_ont, s_onr, s_pj = sem("s_ot"), sem("s_otok"), sem("s_ont"), sem("s_onr"), sem("s_pj")
        s_fc1, s_y, s_lg, s_vt = sem("s_fc1"), sem("s_y"), sem("s_lg"), sem("s_vt")
        a_si, a_gt, a_ht, a_p1, a_qt = sem("a_si"), sem("a_gt"), sem("a_ht"), sem("a_p1"), sem("a_qt")
        a_sq, a_exp, a_v, a_ot, a_ont = sem("a_sq"), sem("a_exp"), sem("a_v"), sem("a_ot"), sem("a_ont")
        a_gelu, a_vt = sem("a_gelu"), sem("a_vt")
        d_set, d_wa, d_ws, d_mod, d_stat = sem("d_set"), sem("d_wa"), sem("d_ws"), sem("d_mod"), sem("d_stat")
        d_mv, d_xn, d_hm, a_ha, d_hr = sem("d_mv"), sem("d_xn"), sem("d_hm"), sem("a_ha"), sem("d_hr")
        d_r1, d_p2, d_sm, d_mt, d_rec = sem("d_r1"), sem("d_p2"), sem("d_sm"), sem("d_mt"), sem("d_rec")
        d_on, a_oa, d_onr, d_gate, d_ss = sem("d_on"), sem("a_oa"), sem("d_onr"), sem("d_gate"), sem("d_ss")
        d_nw, d_qn, d_top, d_cw, d_y = sem("d_nw"), sem("d_qn"), sem("d_top"), sem("d_cw"), sem("d_y")
        d_rep, d_xr, a_ox = sem("d_rep"), sem("d_xr"), sem("a_ox")
        g_zero, g_set, g_ra, g_rb, g_rc = sem("g_zero"), sem("g_set"), sem("g_ra"), sem("g_rb"), sem("g_rc")
        g_rd, g_rs, g_p3, g_x, g_ew = sem("g_rd"), sem("g_rs"), sem("g_p3"), sem("g_x"), sem("g_ew")
        alone = sem("alone")

        block = ctx.enter_context(nc.Block())

        chunks = [("qkv", 0), ("proj", 0), ("gate", 0)] + [("fc1", L - 1 + e) for e in range(E)]
        for l in range(1, L):
            chunks += [("qkv", l), ("proj", l)]
        NEAR = 2
        EARLY = len(chunks)
        chunks += [("fc1", l - 1) for l in range(1, L)]
        WIDTH = {"qkv": 3 * C, "proj": C, "fc1": HID, "gate": E}
        SPLIT = {"qkv": rqkv, "proj": rproj, "fc1": rfc1}

        times = [(6, 0, 1), (6, 0, 3), (6, 1, 1), (6, 2, 1), (7, 0, 1), (7, 0, 3), (7, 1, 1), (7, 1, 3), (7, 2, 0),
                 (7, 2, 2), (7, 3, 0)]
        SPLIT_AT = dict(zip(times, range(NEAR, EARLY)))

        def slot(what, k):
            return k - (L - 1) if what == "fc1" and k >= L - 1 else k

        def staged(i):
            return i % NST if i < EARLY else i - EARLY

        def written(l, n):
            return 64 * (n + 1) if l < 3 else 64 * 24 + 192 * (n + 1 - 24)

        def read(l, pair):
            return 96 * (4 * l + pair + 1) if l < 3 else 96 * 12 + 144 * (pair + 1)

        def fc1_slot(l, e):
            return e if l == 0 else l - 1

        fc1_base = [8 * sum(FC1_OF[:l]) for l in range(L + 1)]
        y_base = [8 * sum(Y_OF[:l]) for l in range(L + 1)]

        @block.sync
        def _(sp):
            def load_chunk(i):
                what, k = chunks[i]
                n = WIDTH[what]
                done = q_st[i % NST] if i < EARLY else q_late[i - EARLY]
                if NST <= i < EARLY:
                    sp.wait_ge(d_ws, CR + i - NST + 1)
                src, bias = io.rest(what, k)
                sp.dma_start(stage[0:4 * CR_CH, staged(i), 0:n], src.unsqueeze(0).to_broadcast([4, CR_CH, n])) \
                    .then_inc(done, 16)
                if bias is not None:
                    sp.dma_start(stage[4 * CR_CH:REM, staged(i), 0:n], bias.unsqueeze(0).to_broadcast([2, n])) \
                        .then_inc(done, 16)

            sp.dma_start(si[:], io.cT[0:CM]).then_inc(q_c, 16)
            sp.wait_ge(d_set, CR + 1)
            sp.dma_start(sir[0:CR_CH], io.cT[CM:C]).then_inc(q_c, 16)
            sp.dma_start(ident[:], io.ident).then_inc(q_c, 16)
            sp.dma_start(masks[:], io.masks).then_inc(q_c, 16)
            sp.dma_start(maskf[:], io.block_mask).then_inc(q_c, 16)
            for i, a in enumerate(io.gains):
                sp.dma_start(gains[:, i:i + 1], a.unsqueeze(0).to_broadcast([128, 1])).then_inc(q_c, 16)
            sp.dma_start(ada[:, 0, :], io.ada_w[0][0:CM, :]).then_inc(q_ada[0], 16)
            sp.dma_start(adar[0:CR_CH, 0, :], io.ada_w[0][CM:C, :]).then_inc(q_ada[0], 16)
            sp.dma_start(adar[CR_CH:CR_CH + 1, 0, :], io.ada_b[0].unsqueeze(0)).then_inc(q_ada[0], 16)
            xv = io.x.rearrange("b t c -> t b c")
            sp.dma_start(X[:, 0:2 * G, :], xv[:, 0:2 * G, :]).then_inc(q_x0, 16)
            sp.dma_start(wqkv[:, 0, :], io.qkv_w[0][0:CM, :]).then_inc(q_w0, 16)
            sp.dma_start(wproj[:, 0, :], io.proj_w[0][0:CM, :]).then_inc(q_w0, 16)
            for i in range(NEAR):
                load_chunk(i)
            for l in range(1, L):
                sp.dma_start(ada[:, l, :], io.ada_w[l][0:CM, :]).then_inc(q_ada[l], 16)
                sp.dma_start(adar[0:CR_CH, l, :], io.ada_w[l][CM:C, :]).then_inc(q_ada[l], 16)
                sp.dma_start(adar[CR_CH:CR_CH + 1, l, :], io.ada_b[l].unsqueeze(0)).then_inc(q_ada[l], 16)
            sp.dma_start(X[:, 2 * G:B, :], xv[:, 2 * G:B, :]).then_inc(q_x1, 16)
            for l in range(L):
                sp.wait_ge(a_gt, CR + l + 1)
                sp.dma_start(gate_scr[l].rearrange("w b c -> b w c"), gsb[:, l, :].rearrange("b (w c) -> b w c", w=2)) \
                    .then_inc(q_gs, 16)
            for i in range(NEAR, NST + NEAR):
                load_chunk(i)

            def far_weights():
                for l in range(1, L):
                    sp.dma_start(wqkv[:, l, :], io.qkv_w[l][0:CM, :]).then_inc(q_w1, 16)
                    sp.dma_start(wproj[:, l, :], io.proj_w[l][0:CM, :]).then_inc(q_w1, 16)
                sp.dma_start(wgate[:], io.gate_w[0:CM, :]).then_inc(q_w1, 16)
                for e in range(E):
                    load_mlp(L - 1 + e, q_w1)

            def load_mlp(k, done):
                w1, w2, b2 = io.mlp(k)
                at = slot("fc1", k)
                sp.dma_start(wfc1[:, at, :], w1[0:CM, :]).then_inc(done, 16)
                sp.dma_start(wfc2[:, at, 0:KT - 1, :], w2[0:128 * (KT - 1), :].rearrange("(k p) c -> p k c", p=128)) \
                    .then_inc(done, 16)
                sp.dma_start(wfc2[0:TAIL, at, KT - 1, :], w2[128 * (KT - 1):HID, :]).then_inc(done, 16)
                sp.dma_start(wfc2[TAIL:TAIL + 1, at, KT - 1, :], b2.unsqueeze(0)).then_inc(done, 16)

            def late_weights():
                sp.wait_ge(s_y, CR + y_base[1])
                for i in range(EARLY, len(chunks)):
                    load_chunk(i)
                for l in range(1, L):
                    load_mlp(l - 1, q_w2)

            def load_gates(l, w, g, p, n1):
                sp.wait_ge(d_gate, CR + 2 * n1 - 2)
                sp.dma_start(gbuf[:, p, :, :].rearrange("t b c -> t (b c)"),
                             gate_scr[l, w, bass.ds(G * g, G), :].rearrange("b c -> (b c)").unsqueeze(0)
                             .to_broadcast([T, G * C])).then_inc(q_g[p], 16)

            def write_parts(l, n, p):
                for m in range(3):
                    sp.wait_ge(a_p1, CR + 3 * n + m + 1)
                    sp.wait_ge(d_p2, CR + 3 * n + m + 1)
                    sp.wait_ge(g_p3, CR + 3 * n + m + 1)
                    for side in range(2):
                        a = max(0, QK_DIMS * m - D * side)
                        b = min(D, QK_DIMS * (m + 1) - D * side)
                        if a >= b:
                            continue
                        r0 = H * (a + D * side) - QK_ROWS * m
                        src = parts[r0:r0 + H * (b - a), m]
                        if l < 3:
                            sp.dma_start(qk_scr[p, side, :, a:b].rearrange("a d h t -> (d h) a t"), src).then_inc(q_w, 16)
                            continue
                        for part in range(3):
                            sp.dma_start(tok_scr[p, side, :, part, a:b].rearrange("b d h t -> (d h) b t"),
                                         src[:, part].rearrange("r (b t) -> r b t", b=G)).then_inc(q_w, 16)
                if l == 3:
                    for m in range(2):
                        sp.wait_ge(a_vt, CR + 2 * (n - 24) + m + 1)
                        sp.dma_start(v_scr[p, :, 6 * m:6 * m + TOK_V[m] // H].rearrange("b d h t -> (d h) b t"),
                                     vt[m].rearrange("r (b t) -> r b t", b=G)).then_inc(q_vw, 16)

            def read_parts(l, n, p):
                sp.wait_ge(s_st, CR + 16 * (n - 1))
                sp.wait_ge(q_w, written(l, n))
                for s in range(2):
                    r0 = 64 * s
                    for part in range(3):
                        rows = (3 - part) * D
                        if l < 3:
                            q_src, k_src = (qk_scr[p, side, :, :, 8 * s:8 * s + 8].rearrange("a d h t -> (a d) (h t)")
                                            for side in range(2))
                            q_dst = qq[r0:r0 + rows, p, s].rearrange("r h t -> r (h t)")
                            k_dst = kk[r0:r0 + rows, p].rearrange("r h t -> r (h t)")
                            sp.dma_start(q_dst, q_src[0:rows]).then_inc(q_r[p][s], 16)
                            sp.dma_start(k_dst, k_src[D * part:D * part + D].unsqueeze(0)
                                         .to_broadcast([3 - part, D, 8 * TG])).then_inc(q_r[p][s], 16)
                        else:
                            bs = slice(2 * s, 2 * s + 2)
                            q_dst = qq[r0:r0 + rows, p, s].rearrange("r h t -> r (h t)").rearrange("r (b x) -> r b x", b=2)
                            k_dst = kk[r0:r0 + rows, p].rearrange("r h t -> r (h t)").rearrange("r (b x) -> r b x", b=2)
                            sp.dma_start(q_dst, tok_scr[p, 0].rearrange("b a d h t -> (a d) b (h t)")[0:rows, bs]) \
                                .then_inc(q_r[p][s], 16)
                            for i in range(3 - part):
                                sp.dma_start(k_dst[D * i:D * i + D],
                                             tok_scr[p, 1, :, part].rearrange("b d h t -> d b (h t)")[:, bs]) \
                                    .then_inc(q_r[p][s], 16)
                        r0 += rows
                if l == 3:
                    sp.wait_ge(s_v, CR + 2 * n)
                    sp.sem_inc(alone, 1)
                    sp.wait_ge(q_vw, 32 * (n + 1 - 24))
                    sp.dma_start(vT, v_scr[p].rearrange("b d h t -> (b d) (h t)")).then_inc(q_vr, 16)

            def attention(l):
                n0, n1 = 8 * l, 16 * l
                if l == 0:
                    sp.wait_ge(q_gs, 16 * L)
                    sp.wait_ge(s_ada, CR + L)
                    sp.wait_ge(d_set, CR + 3)
                    sp.wait_ge(g_set, CR + 4)
                load_gates(l, 0, 0, 0, n1)
                if l == 3:
                    sp.wait_ge(s_st, CR + 16 * n0)
                    for p in range(2):
                        for half in range(2):
                            for side, dst in enumerate((qq[:, p, half], kk[:, p])):
                                r = 64 * half + KS
                                sp.dma_start(dst[r:r + TB].rearrange("r h t -> r (h t)")
                                             .rearrange("r (x t) -> r x t", t=T),
                                             maskb[:, side, :].unsqueeze(1).to_broadcast([TB, 2 * H, T])) \
                                    .then_inc(q_mask, 16)
                write_parts(l, n0, 0)
                read_parts(l, n0, 0)
                write_parts(l, n0 + 1, 1)
                read_parts(l, n0 + 1, 1)
                def step(g, p, f1, nxt):
                    n = n0 + g
                    if nxt:
                        load_gates(l, 0, g + 1, 1 - p, n1 + g + 1)
                    if f1:
                        write_parts(l, n + 2, p)
                        read_parts(l, n + 2, p)

                with sp.Fori(0, 3) as i:
                    step(2 * i, 0, True, True)
                    step(2 * i + 1, 1, True, True)
                if l == 1:
                    late_weights()
                step(6, 0, False, True)
                step(7, 1, False, False)

            def mlp(l):
                n1 = 16 * l + 8
                load_gates(l, 1, 0, 0, n1)

                def step(g, p):
                    if l == L - 1:
                        sp.wait_ge(g_x, CR + 2 * (n1 + g + 1))
                        sp.dma_start(io.out.rearrange("b t c -> t b c")[:, bass.ds(G * g, G), :],
                                     X[:, bass.ds(G * g, G), :]).then_inc(q_out, 16)

                with sp.Fori(0, 3) as i:
                    load_gates(l, 1, 2 * i + 1, 1, n1 + 2 * i + 1)
                    step(2 * i, 0)
                    load_gates(l, 1, 2 * i + 2, 0, n1 + 2 * i + 2)
                    step(2 * i + 1, 1)
                load_gates(l, 1, 7, 1, n1 + 7)
                step(6, 0)
                step(7, 1)

            far_weights()
            for l in range(L):
                attention(l)
                if l == 0:
                    for i in range(NST + NEAR, EARLY):
                        load_chunk(i)
                mlp(l)
            sp.wait_ge(q_out, 16 * NG)

        @block.tensor
        def _(pe):
            for x in (s_ada, s_ht, s_hr, s_qk, s_qt, s_v, s_sm, s_mt, s_st, s_pv, s_ot, s_otok, s_ont, s_onr,
                      s_pj, s_fc1, s_y, s_lg, s_vt):
                pe.sem_inc(x, CR)

            def layer_mods(l):
                pe.wait_ge(q_ada[l], 48)
                pe.wait_ge(d_rep, CR + l + 1)
                if l >= 2:
                    pe.wait_ge(d_mod, CR + l - 1)
                    pe.wait_ge(a_gt, CR + l - 1)
                o = 3 * (l % 2)
                for k, col in enumerate((0, C, 3 * C, 4 * C)):
                    pe.matmul(bank[o][:, B * k:B * k + B], ada[:, l, col:col + CM], si[:], start=True, stop=False)
                    pe.matmul(bank[o][:, B * k:B * k + B], adar[:, l, col:col + CM], sir[:], start=False, stop=True)
                for k in range(4):
                    out = bank[o + 1][0:REM - 2, B * k:B * k + B]
                    pe.matmul(out, ada4[:, 2 * (l % 2), k, :], si[:], start=True, stop=False)
                    pe.matmul(out, ada4[0:CR_CH + 1, 2 * (l % 2) + 1, k, :], sir[:], start=False, stop=True)
                for k, col in enumerate((2 * C, 5 * C)):
                    pe.matmul(bank[o + 2][0:B, C * k:C * k + C], si[:], ada[:, l, col:col + C], start=True, stop=False)
                    mm = pe.matmul(bank[o + 2][0:B, C * k:C * k + C], sir[:], adar[:, l, col:col + C],
                                   start=False, stop=True)
                mm.then_inc(s_ada, 1)

            def t_main(n1, p, o):
                pe.wait_ge(d_xn, CR + 4 * (n1 + 1))
                for b in range(G):
                    mm = pe.transpose(bank[o][:, T * b:T * b + T], xn[:, p, b, 0:CM], ident[:])
                mm.then_inc(s_ht, 1)

            def t_rem(n1, p, o):
                pe.wait_ge(d_xr, CR + n1 + 1)
                pe.sem_inc(alone, 1)
                for b in range(G):
                    mm = pe.transpose(bank[o][0:REM - 2, T * b:T * b + T],
                                      xr[:, p, b].rearrange("t r c -> t (r c)"), ident[:])
                mm.then_inc(s_hr, 1)

            def q_and_k_by_token(l, n, n1, p, where):
                pe.wait_ge(a_ht, CR + 4 * (n1 + 1))
                pe.wait_ge(d_hr, CR + n1 + 1)
                for b, o in where:
                    if o == 2:
                        pe.wait_ge(a_qt, CR + 4 * (n - 16) + b)
                    pe.matmul(bank[o][:, 0:2 * C], hT[:, p, T * b:T * b + T], wqkv[:, l, 0:2 * C],
                              start=True, stop=False)
                    pe.matmul(bank[o][:, 0:2 * C], hr[:, p, T * b:T * b + T], rqkv[:, l, 0:2 * C],
                              start=False, stop=True).then_inc(s_qt, 1)

            def q_and_k(l, n, n1, p, where):
                if l == 2:
                    pe.wait_ge(a_qt, CR + 4 * (n - 16 + 1))
                    for m, o in where:
                        pe.wait_ge(d_qn, CR + 8 * (n - 16) + (8 if m else 4))
                        if o == 2:
                            pe.wait_ge(d_r1, CR + 3 * n + m)
                        for b in range(G):
                            mm = pe.transpose(bank[o][0:QK_ROWS, T * b:T * b + T],
                                              qs[:, b, QK_ROWS * m:QK_ROWS * m + QK_ROWS], ident[:])
                        mm.then_inc(s_qk, 1)
                    return
                pe.wait_ge(a_ht, CR + 4 * (n1 + 1))
                pe.wait_ge(d_hr, CR + n1 + 1)
                for m, o in where:
                    cols = slice(QK_ROWS * m, QK_ROWS * m + QK_ROWS)
                    out = bank[o][0:QK_ROWS, :]
                    if o == 2 and m > 0 and len(where) == 1:
                        pe.wait_ge(d_r1, CR + 3 * n + m)
                    pe.matmul(out, wqkv[:, l, cols], hT[:, p, :], start=True, stop=False)
                    pe.matmul(out, rqkv[:, l, cols], hr[:, p, :], start=False, stop=True).then_inc(s_qk, 1)

            def values_t(p, m):
                cols = slice(2 * C + TOK_V[0] * m, 2 * C + TOK_V[0] * m + TOK_V[m])
                out = bank[3 + m][0:TOK_V[m], :]
                pe.matmul(out, wqkv[:, 3, cols], hT[:, p, :], start=True, stop=False)
                pe.matmul(out, rqkv[:, 3, cols], hr[:, p, :], start=False, stop=True).then_inc(s_vt, 1)

            def values(l, p, q):
                if l == 3:
                    for i in range(H // 2):
                        mm = pe.transpose(bank[3 + q][:, G * D * i:G * D * i + G * D],
                                          vT[:, H // 2 * q + i:H * T:H], ident[0:G * D, 0:G * D])
                    mm.then_inc(s_v, 1)
                    return
                for b in (2 * q, 2 * q + 1):
                    out = bank[3 + q][:, C * (b % 2):C * (b % 2) + C]
                    pe.matmul(out, hT[:, p, T * b:T * b + T], wqkv[:, l, 2 * C:3 * C], start=True, stop=False)
                    mm = pe.matmul(out, hr[:, p, T * b:T * b + T], rqkv[:, l, 2 * C:3 * C], start=False, stop=True)
                mm.then_inc(s_v, 1)

            def operand(l, side, p, b, h, rows):
                s = h // 8 if l < 3 else b // 2
                tile = qq[0:rows, p, s] if side == 0 else kk[0:rows, p]
                if l < 3:
                    return tile[:, h % 8, T * b:T * b + T]
                at = H * T * (b % 2)
                return tile.rearrange("r h t -> r (h t)")[:, at + h:at + H * T:H]

            def scores_for_max(l, u, b, p, c):
                pe.wait_ge(d_sm, CR + 4 * u + c - 1)
                for i in range(4):
                    h = 4 * c + i
                    mm = pe.matmul(bank[3 + c % 2][:, T * i:T * i + T], operand(l, 0, p, b, h, 127),
                                   operand(l, 1, p, b, h, 127), start=True, stop=True)
                mm.then_inc(s_sm, 1)

            def turn_max(u, up):
                pe.wait_ge(d_sm, CR + 4 * (u + 1))
                pe.wait_ge(d_mt, CR + u)
                pe.transpose(bank[7][:].bitcast(BF16)[0:H, 0:T], negm[:, up, :], identb[:]).then_inc(s_mt, 1)

            def scores(l, K, b, p, c):
                for i in range(4):
                    h = 4 * c + i
                    mm = pe.matmul(bank[c % 2][:, T * i:T * i + T], operand(l, 1, p, b, h, 128),
                                   operand(l, 0, p, b, h, 128), start=True, stop=True)
                mm.then_inc(s_st, 1)

            def weigh(K, nb, b, p, c):
                pe.wait_ge(a_exp, CR + K + 1)
                if c % 2 == 0:
                    pe.wait_ge(a_ot, CR + 2 * nb - 1 + c // 2)
                if c == 2 and b == 0:
                    pe.wait_ge(d_gate, CR + weigh.gates)
                if c == 0:
                    if b == 0:
                        pe.wait_ge(d_onr, CR + weigh.n)
                for i in range(4):
                    h = 4 * c + i
                    mm = pe.matmul(bank[6 - c // 2][32 * i:32 * i + 32, T * (c % 2):T * (c % 2) + T], V[:, p, b, VS * h:VS * h + 32],
                                   prob[:, c, T * i:T * i + T], start=True, stop=True)
                mm.then_inc(s_pv, 1)

            def to_tokens(nb, par):
                pe.wait_ge(a_ot, CR + 2 * (nb + 1))
                pe.wait_ge(d_on, CR + nb)
                for c in range(4):
                    mm = pe.transpose(bank[7][:, T * c:T * c + T], OT[:, par, T * c:T * c + T], ident[:])
                mm.then_inc(s_otok, 1)

            def turn_back(n):
                pe.wait_ge(d_on, CR + 4 * (n + 1))
                for b in range(G):
                    mm = pe.transpose(bank[7][:, T * b:T * b + T], On[:, b, 0:CM], ident[:])
                mm.then_inc(s_ont, 1)
                pe.wait_ge(a_ox, CR + n + 1)
                pe.sem_inc(alone, 1)
                for b in range(G):
                    mm = pe.transpose(bank[6][0:REM - 2, T * b:T * b + T],
                                      Onr[:, b].rearrange("t r c -> t (r c)"), ident[:])
                mm.then_inc(s_onr, 1)

            def project(l, n):
                pe.wait_ge(a_ont, CR + n + 1)
                def main(b):
                    pe.matmul(bank[5 + 2 * (b // 2)][:, C * (b % 2):C * (b % 2) + C], OnT[:, T * b:T * b + T],
                              wproj[:, l, :], start=True, stop=False)

                def rest(b):
                    return pe.matmul(bank[5 + 2 * (b // 2)][:, C * (b % 2):C * (b % 2) + C], onr[:, T * b:T * b + T],
                                     rproj[:, l, :], start=False, stop=True)

                main(0)
                main(2)
                pe.wait_ge(d_onr, CR + n + 1)
                rest(0)
                main(1)
                rest(1).then_inc(s_pj, 1)
                rest(2)
                main(3)
                rest(3).then_inc(s_pj, 1)

            def attention(l):
                n0, m0 = 8 * l, 16 * l
                if l == 0:
                    pe.wait_ge(q_w0, 32)
                    pe.wait_ge(d_ws, CR + NEAR)
                    pe.wait_ge(d_mod, CR + L)
                    pe.wait_ge(a_gt, CR + L)
                    pe.wait_ge(g_set, CR + 1)
                    pe.wait_ge(d_set, CR + 2)
                else:
                    pe.wait_ge(a_gelu, CR + fc1_base[l])
                    pe.wait_ge(d_gate, CR + 2 * m0)
                for g in range(2):
                    if g == 1:
                        pe.wait_ge(d_r1, CR + 3 * n0 + 3)
                        if l == 2:
                            pe.wait_ge(a_v, CR + 2 * (n0 + 1))
                    if g or l == 0:
                        t_main(m0 + g, g, 2)
                        t_rem(m0 + g, g, 5)
                    if l == 2:
                        q_and_k_by_token(l, n0 + g, m0 + g, g, ((0, 0), (1, 1), (2, 3), (3, 4)))
                    q_and_k(l, n0 + g, m0 + g, g, ((0, 0), (1, 1), (2, 2)))
                    if l == 3:
                        pe.wait_ge(a_vt, CR + 2 * g)
                        values_t(g, 0)
                        values_t(g, 1)
                    elif g == 0:
                        if l == 2:
                            pe.wait_ge(a_qt, CR + 4)
                        values(l, 0, 0)
                        values(l, 0, 1)
                if l == 3:
                    pe.wait_ge(a_vt, CR + 4)
                    pe.wait_ge(q_vr, 16)
                    values(l, 0, 0)
                    values(l, 0, 1)
                    pe.wait_ge(q_mask, 16 * 8)
                pe.wait_ge(a_v, CR + 2 * (n0 + 1))
                pe.wait_ge(d_hm, CR + 4 * (m0 + 2))
                if l == 2:
                    pe.wait_ge(a_qt, CR + 8)
                for s in range(2):
                    pe.wait_ge(q_r[0][s], read(l, 0))
                for j in range(3):
                    for c in range(4 if j < 2 else 2):
                        scores_for_max(l, 4 * n0 + j, j, 0, c)
                    if j < 2 and l < 3:
                        turn_max(4 * n0 + j, j)
                pe.wait_ge(d_r1, CR + 3 * (n0 + 2))
                pe.wait_ge(q_m[0], 16 * (2 * n0 + 1))
                for c in range(2):
                    scores(l, 16 * n0 + c, 0, 0, c)

                def step(g, p, f1, nxt):
                    n, n1 = n0 + g, m0 + g
                    weigh.n, weigh.gates = n, 2 * n1
                    pair = g // 2 if isinstance(g, int) else step.i
                    for j in range(G):
                        nb = 4 * n + j
                        for c in range(4):
                            K = 4 * nb + c
                            if c < 2 or j < G - 1 or nxt:
                                if c == 2:
                                    pe.wait_ge(q_m[(j + 1) % 2], 16 * (2 * n + (j + 1) // 2 + 1))
                                pe.wait_ge(a_exp, CR + K + 1)
                                b, q = (j, p) if c < 2 else (j + 1, p) if j < G - 1 else (0, 1 - p)
                                scores(l, K + 2, b, q, (c + 2) % 4)
                            weigh(K, nb, j, p, c)
                            if c == 2 and l < 3 and (j < 2 or nxt):
                                if j == 0:
                                    pe.wait_ge(d_gate, CR + 2 * n1)
                                elif j > 1:
                                    pe.wait_ge(d_on, CR + nb - 1)
                                turn_max(nb + 2, j % 2)
                            if nxt and (j, c) == (1, 2):
                                for half in range(2):
                                    pe.wait_ge(q_r[1 - p][half], read(l, pair + p))
                            ahead, cm = (j + 2, c + 2) if c < 2 else (j + 3, c - 2)
                            if ahead < G:
                                scores_for_max(l, 4 * n + ahead, ahead, p, cm)
                            elif nxt:
                                scores_for_max(l, 4 * n + ahead, ahead - G, 1 - p, cm)
                            if (j, c) == ((0, 1) if l == 2 else (0, 3)) and f1:
                                pe.wait_ge(d_r1, CR + 3 * (n + 2))
                                t_rem(n1 + 2, p, 2)
                            if (j, c) == ((1, 0) if l == 2 else (1, 1)) and f1:
                                pe.wait_ge(d_hm, CR + 4 * (n1 + 3))
                                t_main(n1 + 2, p, 2)
                            if not nxt and (j, c) == (0, 3):
                                pe.wait_ge(d_r1, CR + 3 * (n0 + 8))
                                t_rem(m0 + 8, 0, 2)
                            if not nxt and (j, c) == (1, 1):
                                pe.wait_ge(d_hm, CR + 4 * (m0 + 9))
                                t_main(m0 + 8, 0, 2)
                            if f1 and l != 2 and (j, c) in ((2, 1), (3, 0)):
                                q_and_k(l, n + 2, n1 + 2, p, ((j - 2, 2),))
                            if f1 and l == 2 and (j, c) in BY_TOKEN:
                                q_and_k_by_token(l, n + 2, n1 + 2, p, ((BY_TOKEN.index((j, c)), 2),))
                            if f1 and l == 2 and (j, c) in TURNED:
                                q_and_k(l, n + 2, n1 + 2, p, ((TURNED.index((j, c)), 2),))
                            if c == 3 and j > 0:
                                if l < 3 and (j < 2 or nxt):
                                    pe.wait_ge(d_mt, CR + nb + 3)
                                elif l == 3 and j == 1:
                                    pe.wait_ge(d_gate, CR + 2 * n1)
                                to_tokens(nb - 1, (j - 1) % 2)
                    if f1:
                        q_and_k(l, n + 2, n1 + 2, p, ((2, 2),))
                    to_tokens(4 * n + 3, 1)
                    if nxt:
                        pe.wait_ge(d_sm, CR + 4 * (4 * n + 6) + 2)
                        for q in range(2):
                            if l < 3:
                                values(l, 1 - p, q)
                            elif f1:
                                values_t(p, q)
                    turn_back(n)
                    if nxt and l == 3:
                        if f1:
                            pe.wait_ge(a_vt, CR + 2 * (n - 24 + 3))
                            pe.sem_inc(alone, 1)
                        pe.wait_ge(q_vr, 16 * (n - 24 + 2))
                        pe.sem_inc(alone, 1)
                        values(l, 1 - p, 0)
                        values(l, 1 - p, 1)
                    project(l, n)
                    if nxt:
                        pe.wait_ge(a_v, CR + 2 * (n + 2))

                with pe.Fori(0, 2) as i:
                    step.i = i
                    step(2 * i, 0, True, True)
                    step(2 * i + 1, 1, True, True)
                step(4, 0, True, True)
                step(5, 1, True, True)
                step(6, 0, False, True)
                step(7, 1, False, False)

            def mlp(l):
                m0 = 16 * l + 8
                n_last = 8 * (l + 1)
                if l == 0:
                    pe.wait_ge(q_w1, 16 * (2 * (L - 1) + 1 + 4 * E))
                    pe.wait_ge(d_ws, CR + EARLY + 1)
                if l == 1:
                    pe.wait_ge(q_w2, 16 * 4 * (L - 1))
                    pe.wait_ge(d_ws, CR + len(chunks) + 1)
                pe.wait_ge(a_exp, CR + 16 * n_last)
                pe.wait_ge(d_gate, CR + 2 * m0)
                pe.wait_ge(d_onr, CR + n_last)

                def first(e, f0):
                    for m in range(KT):
                        rows = min(128, HID - 128 * m)
                        cols = slice(128 * m, 128 * m + rows)
                        k = fc1_slot(l, e)
                        out = bank[2 + m % 3][0:rows, :]
                        if m < 3:
                            pe.wait_ge(a_gelu, CR + f0)
                        else:
                            pe.wait_ge(a_gelu, CR + f0 + m - 2)
                        pe.matmul(out, wfc1[:, k, cols], hT[:, first.p, :], start=True, stop=False)
                        pe.matmul(out, rfc1[:, k, cols], hr[:, first.p, :], start=False, stop=True) \
                            .then_inc(s_fc1, 1)

                def second(e, f0, y0, n1):
                    k = fc1_slot(l, e)
                    for q in range(2):
                        if l == 0:
                            pe.wait_ge(d_y, CR + y0 + q - 1)
                        else:
                            pe.wait_ge(d_gate, CR + 2 * n1 + q - 1)
                        for b in (2 * q, 2 * q + 1):
                            out = bank[5 + q][:, C * (b % 2):C * (b % 2) + C]
                            for t in range(KT):
                                if q == 0 and b == 0:
                                    pe.wait_ge(a_gelu, CR + f0 + t + 1)
                                rows = 128 if t < KT - 1 else TAIL + 1
                                mm = pe.matmul(out, hid[0:rows, t, T * b:T * b + T], wfc2[0:rows, k, t, :],
                                               start=(t == 0), stop=(t == KT - 1))
                        mm.then_inc(s_y, 1)

                def gate_logits(p):
                    for b in range(G):
                        out = bank[7][:, E * b:E * b + E]
                        pe.matmul(out, hT[:, p, T * b:T * b + T], wgate[:], start=True, stop=False)
                        mm = pe.matmul(out, hr[0:REM - 2, p, T * b:T * b + T], rgate[:], start=False, stop=True)
                    mm.then_inc(s_lg, 1)

                def step(g, p, nxt):
                    n1 = m0 + g
                    first.p = p
                    pe.wait_ge(a_ht, CR + 4 * (n1 + 1))
                    pe.wait_ge(d_hr, CR + n1 + 1)
                    if l == 0:
                        pe.wait_ge(d_top, CR + 2 * g)
                        gate_logits(p)
                    for e in range(E if l == 0 else 1):
                        f0 = fc1_base[l] + FC1_OF[l] * g + KT * e
                        first(e, f0)
                        if e == 0 and (nxt or l < L - 1):
                            t_main(n1 + 1, 1 - p, 0)
                            t_rem(n1 + 1, 1 - p, 1)
                        second(e, f0, y_base[l] + Y_OF[l] * g + 2 * e, n1)

                with pe.Fori(0, 3) as i:
                    step(2 * i, 0, True)
                    step(2 * i + 1, 1, True)
                step(6, 0, True)
                step(7, 1, False)

            pe.wait_ge(q_c, 16 * 9)
            pe.wait_ge(a_si, CR + 2)
            for l in range(L):
                layer_mods(l)
            for l in range(L):
                attention(l)
                mlp(l)

        @block.scalar
        def _(act):
            for x in (a_si, a_gt, a_ht, a_p1, a_qt, a_sq, a_exp, a_v, a_ot, a_ont, a_gelu, a_vt, a_ha, a_oa,
                      a_ox):
                act.sem_inc(x, CR)

            def mod_main(l, which, g, p, n1, o):
                act.wait_ge(s_ht, CR + n1 + 1)
                for b in range(G):
                    at = bass.ds(G * g + b, 1)
                    act.activation(hT[:, p, T * b:T * b + T], bank[o][:, T * b:T * b + T], ACT.Identity,
                                   scale=modm[:, l, 2 * which + 1, at], bias=modm[:, l, 2 * which, at]) \
                        .then_inc(a_ht, 1)

            def round_rem(n1):
                act.wait_ge(d_hm, CR + 4 * (n1 + 1))
                act.wait_ge(d_hr, CR + n1)
                act.activation(hhi[:], hmod[:], ACT.Copy).then_inc(a_ha, 1)

            def part1(l, n, q_reuse, tiles=range(3), bank_of=lambda m: m):
                for m in tiles:
                    act.wait_ge(s_qk, CR + 3 * n + m + 1)
                    if m == 0 and q_reuse:
                        act.wait_ge(q_w, written(l, n - 1))
                    act.activation(parts[:, m, 0, :], bank[bank_of(m)][0:QK_ROWS, :], ACT.Copy).then_inc(a_p1, 1)

            def values_t_out(n, q_reuse):
                for m, rows in enumerate(TOK_V):
                    act.wait_ge(s_vt, CR + 2 * (n - 24) + m + 1)
                    if m == 0 and q_reuse:
                        act.wait_ge(q_vw, 32 * (n - 24))
                    act.activation(vt[m], bank[3 + m][0:rows, :], ACT.Copy).then_inc(a_vt, 1)

            def head_squares(n, where):
                for b, o in where:
                    r = 4 * (n - 16) + b
                    act.wait_ge(s_qt, CR + r + 1)
                    act.wait_ge(d_ss, CR + r - 1)
                    act.activation(sq[:, b % 2, :], bank[o][:, 0:2 * C], ACT.Square).then_inc(a_sq, 1)
                    act.activation(qs[:, b, :], bank[o][:, 0:2 * C], ACT.Copy).then_inc(a_qt, 1)

            def values_out(l, n, p, q):
                act.wait_ge(s_v, CR + 2 * n + q + 1)
                if l == 3:
                    out = V[:, p, :, VS * H // 2 * q:VS * H // 2 * (q + 1)].rearrange("t b (h e) -> t b h e", e=VS)
                    act.activation(out[:, :, :, 0:D], bank[3 + q][:, 0:2 * C].rearrange("t (h b d) -> t b h d", b=G, d=D),
                                   ACT.Copy).then_inc(a_v, 1)
                    return
                out = V[:, p, 2 * q:2 * q + 2, 0:H * VS].rearrange("t b (h e) -> t b h e", e=VS)[:, :, :, 0:D]
                act.activation(out, bank[3 + q][:, 0:2 * C].rearrange("t (b h d) -> t b h d", b=2, h=H), ACT.Copy) \
                    .then_inc(a_v, 1)

            def attention(l):
                n0, m0 = 8 * l, 16 * l
                scale = 3.0 if l == 2 else float(D) ** -0.5
                for g in range(2):
                    if g or l == 0:
                        mod_main(l, 0, g, g, m0 + g, 2)
                        round_rem(m0 + g)
                    if l == 2:
                        head_squares(n0 + g, ((0, 0), (1, 1), (2, 3), (3, 4)))
                    part1(l, n0 + g, n0 + g > 0)
                    if l == 3:
                        values_t_out(n0 + g, g > 0)
                    if g == (l == 3):
                        values_out(l, n0, 0, 0)
                        values_out(l, n0, 0, 1)

                def weighed_out(nb, par, half):
                    act.wait_ge(s_pv, CR + 4 * nb + 2 * half + 2)
                    act.wait_ge(s_otok, CR + nb - 1)
                    cols = slice(2 * T * half, 2 * T * half + 2 * T)
                    act.activation(OT[:, par, cols], bank[6 - half][:, 0:2 * T], ACT.Copy).then_inc(a_ot, 1)

                def write_max(u, up, b, p):
                    row = qq[127:128, p].rearrange("r s h t -> r (s h) t")
                    if l < 3:
                        act.wait_ge(d_mt, CR + u + 1)
                        act.dma_start(row[:, :, T * b:T * b + T], mT[:, up, :]).then_inc(q_m[up], 16)
                    else:
                        act.wait_ge(d_sm, CR + 4 * (u + 1))
                        row = row.rearrange("r h t -> r (h t)")[:, H * T * b:H * T * b + H * T]
                        act.dma_start(row.rearrange("r (m t) -> r m t", t=H), negm[:, up, :]).then_inc(q_m[up], 16)

                act.wait_ge(s_st, CR + 16 * n0)
                write_max(4 * n0, 0, 0, 0)
                write_max(4 * n0 + 1, 1, 1, 0)

                def weights(K, c):
                    act.wait_ge(s_st, CR + K + 1)
                    act.wait_ge(s_pv, CR + K - 3)
                    act.activation(prob[:, c, :], bank[c % 2][:], ACT.Exp, scale=scale).then_inc(a_exp, 1)

                for c in range(2):
                    weights(16 * n0 + c, c)

                def step(g, p, f1, nxt):
                    n, n1 = n0 + g, m0 + g
                    for j in range(G):
                        nb = 4 * n + j
                        for c in range(4):
                            if c < 2 or j < G - 1 or nxt:
                                weights(4 * nb + c + 2, (c + 2) % 4)
                            if c == 2:
                                weighed_out(nb, j % 2, 0)
                            if j > 0 and c == 0:
                                weighed_out(nb - 1, (j - 1) % 2, 1)
                            if c == 3 and (j < 2 or nxt):
                                write_max(nb + 2, j % 2, (j + 2) % G, p if j < 2 else 1 - p)
                            if (j, c) == ((0, 3) if l == 2 else (1, 0)) and f1:
                                round_rem(n1 + 2)
                            if (j, c) == ((1, 0) if l == 2 else (1, 2)) and f1:
                                mod_main(l, 0, g + 2, p, n1 + 2, 2)
                            if not nxt and (j, c) == (1, 0):
                                round_rem(m0 + 8)
                            if not nxt and (j, c) == (1, 2):
                                mod_main(l, 1, 0, 0, m0 + 8, 2)
                            if f1 and l != 2 and (j, c) in ((2, 1), (3, 0)):
                                part1(l, n + 2, True, (j - 2,), lambda m: 2)
                            if f1 and l == 2 and (j, c) in BY_TOKEN:
                                head_squares(n + 2, ((BY_TOKEN.index((j, c)), 2),))
                            if f1 and l == 2 and (j, c) in TURNED:
                                part1(l, n + 2, True, (TURNED.index((j, c)),), lambda m: 2)
                    weighed_out(4 * n + 3, 1, 1)
                    if f1:
                        part1(l, n + 2, True, (2,))
                    if nxt and l < 3:
                        values_out(l, n + 1, 1 - p, 0)
                        values_out(l, n + 1, 1 - p, 1)
                    if f1 and l == 3:
                        values_t_out(n + 2, True)
                    act.wait_ge(d_on, CR + 4 * (n + 1))
                    act.activation(Onr[:], On[:, :, CM:C].unsqueeze(2).to_broadcast([T, G, 4, CR_CH]), ACT.Copy) \
                        .then_inc(a_ox, 1)
                    act.wait_ge(s_ont, CR + n + 1)
                    act.activation(OnT[:], bank[7][:], ACT.Copy).then_inc(a_ont, 1)
                    act.wait_ge(s_onr, CR + n + 1)
                    act.wait_ge(d_onr, CR + n)
                    act.activation(ohi[:], bank[6][0:REM - 2, :], ACT.Copy).then_inc(a_oa, 1)
                    if nxt and l == 3:
                        values_out(l, n + 1, 1 - p, 0)
                        values_out(l, n + 1, 1 - p, 1)

                with act.Fori(0, 2) as i:
                    step(2 * i, 0, True, True)
                    step(2 * i + 1, 1, True, True)
                step(4, 0, True, True)
                step(5, 1, True, True)
                step(6, 0, False, True)
                step(7, 1, False, False)

            def mlp(l):
                m0 = 16 * l + 8
                func = ACT.Gelu if l == 3 else ACT.Gelu_apprx_tanh
                if l == 0:
                    act.wait_ge(d_ws, CR + EARLY + 1)

                def step(g, p, nxt):
                    for e in range(E if l == 0 else 1):
                        f0 = fc1_base[l] + FC1_OF[l] * g + KT * e
                        y0 = y_base[l] + Y_OF[l] * g + 2 * e
                        for m in range(KT):
                            rows = min(128, HID - 128 * m)
                            act.wait_ge(s_fc1, CR + f0 + m + 1)
                            if m == 0:
                                act.wait_ge(s_y, CR + y0)
                            act.activation(hid[0:rows, m, :], bank[2 + m % 3][0:rows, :], func) \
                                .then_inc(a_gelu, 1)
                        if e == 0 and nxt:
                            mod_main(l, 1, g + 1, 1 - p, m0 + g + 1, 0)
                            round_rem(m0 + g + 1)
                        elif e == 0 and l < L - 1:
                            mod_main(l + 1, 0, 0, 1 - p, m0 + g + 1, 0)
                            round_rem(m0 + g + 1)

                with act.Fori(0, 3) as i:
                    step(2 * i, 0, True)
                    step(2 * i + 1, 1, True)
                step(6, 0, True)
                step(7, 1, False)

            act.wait_ge(q_c, 16 * 9)
            act.activation(si[:], si[:], ACT.Silu).then_inc(a_si, 1)
            act.activation(sir[0:CR_CH], sir[0:CR_CH], ACT.Silu).then_inc(a_si, 1)
            for l in range(L):
                act.wait_ge(s_ada, CR + l + 1)
                act.activation(gsb[:, l, :], bank[3 * (l % 2) + 2][0:B, 0:2 * C], ACT.Tanh if l == 2 else ACT.Copy) \
                    .then_inc(a_gt, 1)
            act.wait_ge(d_mod, CR + L)
            act.wait_ge(q_gs, 16 * L)
            for l in range(L):
                attention(l)
                mlp(l)

        @block.vector
        def _(dve):
            for x in (d_set, d_wa, d_ws, d_mod, d_stat, d_mv, d_xn, d_hm, d_hr, d_r1, d_p2, d_sm, d_mt, d_rec,
                      d_on, d_onr, d_gate, d_ss, d_nw, d_qn, d_top, d_cw, d_y, d_rep, d_xr):
                dve.sem_inc(x, CR)
            def split_chunk(i):
                what, k = chunks[i]
                n = WIDTH[what]
                rows = REM - 2 if what == "gate" else REM
                if i < EARLY:
                    dve.wait_ge(q_st[i % NST],
                                sum((16 if chunks[x][0] == "gate" else 32) for x in range(i % NST, i + 1, NST)))
                else:
                    dve.wait_ge(q_late[i - EARLY], 32)
                st = stage[0:rows, staged(i), 0:n]
                out = rgate[:] if what == "gate" else SPLIT[what][:, slot(what, k), :]
                dve.wait_ge(d_ws, CR + (i if i < EARLY else i + 1))
                dve.tensor_copy(wtmp[0:rows, 0:n], st).then_inc(d_wa, 1)
                dve.wait_ge(d_wa, CR + i + 1)
                dve.scalar_tensor_tensor(out, wtmp[0:rows, 0:n].bitcast(F32), masks[0:rows, 1:2], st,
                                         ALU.mult, ALU.add).then_inc(d_ws, 1)

            def stats(l, which, g, p, n1):
                if not (l == 0 and which == 0):
                    dve.wait_ge(g_x, CR + 2 * (n1 - 7))
                dve.wait_ge(d_mv, CR + 4 * n1)
                for b in range(G):
                    dve.bn_stats(stat[:, b, :], X[:, bass.ds(G * g + b, 1), :].rearrange("t b c -> t (b c)")) \
                        .then_inc(d_stat, 1)
                dve.wait_ge(g_rs, CR + n1 - 1)
                for b in range(G):
                    dve.wait_ge(d_stat, CR + 4 * n1 + b + 1)
                    dve.sem_inc(alone, 1)
                    dve.bn_aggr(mv[:, p, b, :], stat[:, b, :]).then_inc(d_mv, 1)

            def normalise(l, g, p, n1):
                dve.wait_ge(g_rs, CR + n1 + 1)
                dve.wait_ge(s_hr, CR + n1 - 1)
                for b in range(G):
                    x = X[:, bass.ds(G * g + b, 1), :].rearrange("t b c -> t (b c)")
                    if l == 2:
                        dve.tensor_scalar(xn[:, p, b, :], x, rstd[:, p, b:b + 1], None, ALU.mult) \
                            .then_inc(d_xn, 1)
                    else:
                        dve.tensor_scalar(xn[:, p, b, :], x, mv[:, p, b, 0:1], rstd[:, p, b:b + 1],
                                          ALU.subtract, ALU.mult).then_inc(d_xn, 1)
                dve.wait_ge(d_xn, CR + 4 * (n1 + 1))
                dve.tensor_copy(xr[:, p], xn[:, p, :, CM:C].unsqueeze(2).to_broadcast([T, G, 4, CR_CH])) \
                    .then_inc(d_xr, 1)

            def mod_rem(l, which, g, p, n1, o):
                dve.wait_ge(s_hr, CR + n1 + 1)
                dve.wait_ge(d_hr, CR + n1)
                for b in range(G):
                    at = bass.ds(G * g + b, 1)
                    dve.tensor_scalar(hmod[:, T * b:T * b + T], bank[o][0:REM - 2, T * b:T * b + T],
                                      modr[:, l, 2 * which + 1, at], modr[:, l, 2 * which, at], ALU.mult, ALU.add) \
                        .then_inc(d_hm, 1)

            def split_rem(p, n1):
                dve.wait_ge(a_ha, CR + n1 + 1)
                dve.scalar_tensor_tensor(hr[0:REM - 2, p, :], hhi[:].bitcast(F32), masks[0:REM - 2, 0:1], hmod[:],
                                         ALU.mult, ALU.add).then_inc(d_hr, 1)

            def parts23(l, n, tiles=range(3), bank_of=lambda m: m):
                for m in tiles:
                    i = 3 * n + m
                    dve.wait_ge(a_p1, CR + i + 1)
                    dve.wait_ge(g_p3, CR + (i - 1 if m else i))
                    dve.tensor_tensor(res[:, m % 2, :], bank[bank_of(m)][0:QK_ROWS, :], parts[:, m, 0, :], ALU.subtract) \
                        .then_inc(d_r1, 1)
                    dve.wait_ge(d_r1, CR + i + 1)
                    dve.tensor_copy(parts[:, m, 1, :], res[:, m % 2, :]).then_inc(d_p2, 1)

            def head_sums(n, seqs=range(G)):
                for b in seqs:
                    dve.wait_ge(a_sq, CR + 4 * (n - 16) + b + 1)
                    dve.tensor_reduce(ss[:, b, :].rearrange("t (w h) -> t w h", w=2),
                                      sq[:, b % 2, :].rearrange("t (w d h) -> t w h d", w=2, d=D), AX.X, ALU.add) \
                        .then_inc(d_ss, 1)

            def head_factors(n, steps):
                r = n - 16
                s, y, t = (a[:].rearrange("t b h -> t (b h)") for a in (ss, rs, rt))
                done = CR + 12 * r
                for i in steps:
                    if i == 0:
                        dve.wait_ge(d_ss, CR + 4 * (r + 1))
                        dve.tensor_scalar(s, s, RMS_EPS2, None, ALU.max).then_inc(d_nw, 1)
                        dve.wait_ge(d_nw, done + 1)
                        dve.tensor_scalar(t.bitcast(I32), s.bitcast(I32), 1, None, ALU.arith_shift_right).then_inc(d_nw, 1)
                        dve.wait_ge(d_nw, done + 2)
                        dve.tensor_scalar(y.bitcast(I32), t.bitcast(I32), -1.0, float(MAGIC), ALU.mult, ALU.add) \
                            .then_inc(d_nw, 1)
                        continue
                    dve.wait_ge(d_nw, done + 3 * i)
                    dve.tensor_tensor(t, y, y, ALU.mult).then_inc(d_nw, 1)
                    dve.wait_ge(d_nw, done + 3 * i + 1)
                    dve.scalar_tensor_tensor(t, t, -0.5, s, ALU.mult, ALU.mult).then_inc(d_nw, 1)
                    dve.wait_ge(d_nw, done + 3 * i + 2)
                    dve.scalar_tensor_tensor(y, t, 1.5, y, ALU.add, ALU.mult).then_inc(d_nw, 1)

            def head_norms(n, side):
                r = n - 16
                dve.wait_ge(d_nw, CR + 12 * (r + 1))
                dve.wait_ge(a_qt, CR + 4 * (r + 1))
                for b in range(G):
                    v = qs[:, b, C * side:C * side + C].rearrange("t (d h) -> t d h", d=D)
                    dve.scalar_tensor_tensor(v, v, gains[:, 2 + side:3 + side],
                                             rs[:, b, H * side:H * side + H].unsqueeze(1).to_broadcast([T, D, H]),
                                             ALU.mult, ALU.mult).then_inc(d_qn, 1)

            def head_max(l, u, up, c):
                dve.wait_ge(s_sm, CR + 4 * u + c + 1)
                if l < 3:
                    dve.wait_ge(s_mt, CR + u - 1)
                elif c == 0:
                    dve.wait_ge(q_m[up], head_max.count)
                dve.tensor_reduce(negm[:, up, 4 * c:4 * c + 4], bank[3 + c % 2][:].rearrange("q (h k) -> q h k", k=T),
                                  AX.X, ALU.max, negate=True).then_inc(d_sm, 1)

            def max_out(u, up):
                dve.wait_ge(s_mt, CR + u + 1)
                if not isinstance(u, int) or u >= 2:
                    dve.wait_ge(q_m[up], max_out.count)
                dve.tensor_copy(mT[:, up, :], bank[7][:].bitcast(BF16)[0:H, 0:T]).then_inc(d_mt, 1)

            def attention(l):
                n0, m0 = 8 * l, 16 * l

                def normed(nb, b):
                    dve.wait_ge(s_otok, CR + nb + 1)
                    o = bank[7][:].rearrange("q (h e) -> q h e", e=32)
                    if b == 0:
                        dve.wait_ge(s_onr, CR + normed.n)
                    dve.reciprocal(rec[:, b % 2, :], o[:, :, D]).then_inc(d_rec, 1)
                    dve.wait_ge(d_rec, CR + nb + 1)
                    dve.tensor_tensor(On[:, b, :].rearrange("q (h d) -> q h d", d=D), o[:, :, 0:D],
                                      rec[:, b % 2, :].unsqueeze(2).to_broadcast([T, H, D]), ALU.mult) \
                        .then_inc(d_on, 1)

                def add_back(n, n1, p, q):
                    dve.wait_ge(s_pj, CR + 2 * n + q + 1)
                    dve.wait_ge(g_x, CR + 2 * n1 + q - 1)
                    dve.tensor_tensor(gx[:, q, :, :], bank[5 + 2 * q][:, 0:2 * C].rearrange("t (b c) -> t b c", b=2),
                                      gbuf[:, p, 2 * q:2 * q + 2, :], ALU.mult).then_inc(d_gate, 1)

                first = 0 if l == 0 else 1
                for g in range(first, 2):
                    stats(l, 0, g, g, m0 + g)
                for g in range(first, 2):
                    normalise(l, g, g, m0 + g)
                for g in range(2):
                    if g >= first:
                        mod_rem(l, 0, g, g, m0 + g, 5)
                        split_rem(g, m0 + g)
                    if l == 2:
                        head_sums(n0 + g)
                        head_factors(n0 + g, range(4))
                        for side in range(2):
                            head_norms(n0 + g, side)
                    parts23(l, n0 + g)
                if l == 0:
                    dve.wait_ge(q_x1, 16)
                stats(l, 0, 2, 0, m0 + 2)
                normalise(l, 2, 0, m0 + 2)
                for j in range(3):
                    for c in range(4 if j < 2 else 2):
                        head_max.count = 16 * (2 * n0 + j // 2)
                        head_max(l, 4 * n0 + j, j % 2, c)
                    if j < 2 and l < 3:
                        max_out.count = 16 * (2 * n0 + j // 2)
                        max_out(4 * n0 + j, j % 2)

                def step(g, p, f2, f1, nxt):
                    n, n1 = n0 + g, m0 + g
                    normed.n = n
                    gates = 16 * (8 * l + (g - p) // 2 + 1) if isinstance(g, int) else 16 * (8 * l + step.i + 1)
                    for j in range(G):
                        nb = 4 * n + j
                        head_max.count = 16 * (2 * n + (j + 1) // 2 + 1)
                        for c in range(4):
                            if c == 2 and l < 3 and (j < 2 or nxt):
                                max_out.count = 16 * (2 * n + (j + 2) // 2)
                                max_out(nb + 2, j % 2)
                            ahead, cm = (j + 2, c + 2) if c < 2 else (j + 3, c - 2)
                            if ahead < G or nxt:
                                head_max(l, 4 * n + ahead, ahead % 2, cm)
                            if (j, c) == ((0, 2) if l == 2 else (1, 0)) and f1:
                                mod_rem(l, 0, g + 2, p, n1 + 2, 2)
                            if (j, c) == ((1, 0) if l == 2 else (1, 2)) and f1:
                                split_rem(p, n1 + 2)
                            if (j, c) == ((1, 1) if l == 2 else (1, 3)) and f2:
                                stats(l, 0, g + 3, 1 - p, n1 + 3)
                            if (j, c) == ((2, 1) if l == 2 else (2, 3)) and f2:
                                normalise(l, g + 3, 1 - p, n1 + 3)
                            if l == 0 and not f1 and (g, j, c) in SPLIT_AT:
                                split_chunk(SPLIT_AT[g, j, c])
                            if nxt and not f1 and (j, c) == (1, 3):
                                stats(l, 1, 0, 0, m0 + 8)
                            if nxt and not f1 and (j, c) == (2, 3):
                                normalise(l, 0, 0, m0 + 8)
                            if not nxt and (j, c) == (1, 0):
                                mod_rem(l, 1, 0, 0, m0 + 8, 2)
                            if not nxt and (j, c) == (1, 2):
                                split_rem(0, m0 + 8)
                            if j > 1 and c == 1:
                                normed(nb - 2, j - 2)
                            if f1 and l != 2 and (j, c) in ((2, 2), (3, 1)):
                                parts23(l, n + 2, (j - 2,), lambda m: 2)
                            if f1 and l == 2 and (j, c) in BY_TOKEN_END:
                                head_sums(n + 2, (BY_TOKEN_END.index((j, c)),))
                            if f1 and l == 2 and (j, c) in FACTORS:
                                head_factors(n + 2, FACTORS[j, c])
                            if f1 and l == 2 and (j, c) in NORMS:
                                for side in NORMS[j, c]:
                                    head_norms(n + 2, side)
                            if f1 and l == 2 and (j, c) in TURNED_END:
                                parts23(l, n + 2, (TURNED_END.index((j, c)),), lambda m: 2)
                    normed(4 * n + 2, 2)
                    if f1:
                        parts23(l, n + 2, (2,))
                    normed(4 * n + 3, 3)
                    dve.wait_ge(s_onr, CR + n + 1)
                    dve.wait_ge(a_oa, CR + n + 1)
                    dve.scalar_tensor_tensor(onr[0:REM - 2, :], ohi[:].bitcast(F32), masks[0:REM - 2, 0:1],
                                             bank[6][0:REM - 2, :], ALU.mult, ALU.add).then_inc(d_onr, 1)
                    dve.wait_ge(q_g[p], gates)
                    for q in range(2):
                        add_back(n, n1, p, q)

                with dve.Fori(0, 2) as i:
                    step.i = i
                    step(2 * i, 0, True, True, True)
                    step(2 * i + 1, 1, True, True, True)
                step(4, 0, True, True, True)
                step(5, 1, False, True, True)
                step(6, 0, False, False, True)
                step(7, 1, False, False, False)

            def top2(g, p):
                dve.wait_ge(s_lg, CR + g + 1)
                lv = bank[7][:, 0:G * E].rearrange("t (b e) -> t b e", e=E)
                k0 = 16 * g
                cnt = [0]

                def link(ins):
                    cnt[0] += 1
                    ins.then_inc(d_cw, 1)
                    dve.wait_ge(d_cw, CR + k0 + cnt[0])

                dve.wait_ge(d_y, CR + y_base[0] + Y_OF[0] * g)
                dve.wait_ge(g_ew, CR + g)
                dve.tensor_copy(lg[:], lv).then_inc(d_top, 1)
                dve.wait_ge(d_top, CR + 2 * g + 1)
                link(dve.tensor_reduce(lmax[:], lg[:], AX.X, ALU.max))
                for e in range(E):
                    ins = dve.memset(rank[:, :, e], float(E - 1 - e))
                link(ins)
                for d in range(1, E):
                    lo, hi = slice(0, E - d), slice(d, E)
                    link(dve.tensor_tensor(cmpb[:, :, lo], lg[:, :, lo], lg[:, :, hi], ALU.is_ge))
                    link(dve.tensor_tensor(rank[:, :, lo], rank[:, :, lo], cmpb[:, :, lo], ALU.subtract))
                    link(dve.tensor_tensor(rank[:, :, hi], rank[:, :, hi], cmpb[:, :, lo], ALU.add))
                dve.tensor_tensor(lg[:], lg[:], lmax[:].unsqueeze(2).to_broadcast([T, G, E]), ALU.subtract) \
                    .then_inc(d_top, 1)
                link(dve.tensor_scalar(rank[:], rank[:], 2.0, None, ALU.is_lt))
                dve.wait_ge(g_ew, CR + g + 1)
                link(dve.tensor_tensor(cw[:], cw[:], rank[:], ALU.mult))
                link(dve.tensor_reduce(csum[:], cw[:], AX.X, ALU.add))
                link(dve.reciprocal(csum[:], csum[:]))
                link(dve.tensor_tensor(cw[:], cw[:], csum[:].unsqueeze(2).to_broadcast([T, G, E]), ALU.mult))
                assert cnt[0] == 16

            def mlp(l):
                m0 = 16 * l + 8

                def gated(src, q, n1, p):
                    dve.wait_ge(g_x, CR + 2 * n1 + q - 1)
                    dve.tensor_tensor(gx[:, q, :, :], src, gbuf[:, p, 2 * q:2 * q + 2, :], ALU.mult) \
                        .then_inc(d_gate, 1)

                def step(g, p, nxt, gates):
                    n1 = m0 + g
                    if nxt:
                        stats(l, 1, g + 1, 1 - p, n1 + 1)
                        normalise(l, g + 1, 1 - p, n1 + 1)
                    elif l < L - 1:
                        stats(l + 1, 0, 0, 1 - p, n1 + 1)
                        normalise(l + 1, 0, 1 - p, n1 + 1)
                    if l == 0:
                        top2(g, p)
                    if nxt:
                        mod_rem(l, 1, g + 1, 1 - p, n1 + 1, 1)
                        split_rem(1 - p, n1 + 1)
                    elif l < L - 1:
                        mod_rem(l + 1, 0, 0, 1 - p, n1 + 1, 1)
                        split_rem(1 - p, n1 + 1)
                    y0 = y_base[l] + Y_OF[l] * g
                    if l == 0:
                        dve.wait_ge(d_gate, CR + 2 * n1)
                        for e in range(E):
                            for q in range(2):
                                dve.wait_ge(s_y, CR + y0 + 2 * e + q + 1)
                                if e:
                                    dve.wait_ge(d_y, CR + y0 + 2 * e + q - 1)
                                for b in (2 * q, 2 * q + 1):
                                    y = bank[5 + q][:, C * (b % 2):C * (b % 2) + C]
                                    w = cw[:, b, e:e + 1]
                                    if e == 0:
                                        ins = dve.tensor_scalar(acc[:, b, :], y, w, None, ALU.mult)
                                    else:
                                        ins = dve.scalar_tensor_tensor(acc[:, b, :], y, w, acc[:, b, :],
                                                                       ALU.mult, ALU.add)
                                ins.then_inc(d_y, 1)
                        dve.wait_ge(q_g[p], gates)
                        dve.wait_ge(d_y, CR + y0 + 2 * E)
                        for q in range(2):
                            gated(acc[:, 2 * q:2 * q + 2, :], q, n1, p)
                    else:
                        dve.wait_ge(q_g[p], gates)
                        for q in range(2):
                            dve.wait_ge(s_y, CR + y0 + q + 1)
                            gated(bank[5 + q][:, 0:2 * C].rearrange("t (b c) -> t b c", b=2), q, n1, p)

                with dve.Fori(0, 3) as i:
                    for p in range(2):
                        step(2 * i + p, p, True, 16 * (8 * l + 4 + i + 1))
                step(6, 0, True, 16 * (8 * l + 8))
                step(7, 1, False, 16 * (8 * l + 8))

            def replicate(l):
                dve.wait_ge(q_ada[l], 48)
                dve.wait_ge(s_ada, CR + l - 1)
                for a, src in ((0, ada[:, l, :]), (1, adar[:, l, :])):
                    rows = src.shape[0]
                    src = src.rearrange("p (w s c) -> p w s c", w=2, s=3)
                    for w in range(2):
                        out = ada4[0:rows, 2 * (l % 2) + a, 2 * w:2 * w + 2, :].rearrange("p s (r c) -> p s r c", r=4)
                        ins = dve.tensor_copy(out, src[:, w, 0:2, CM:C].unsqueeze(2).to_broadcast([rows, 2, 4, CR_CH]))
                ins.then_inc(d_rep, 1)

            def take_mods(l):
                o = 3 * (l % 2)
                dve.wait_ge(s_ada, CR + l + 1)
                for out, src in ((modm[:, l], bank[o][:, 0:4 * B]), (modr[:, l], bank[o + 1][0:REM - 2, 0:4 * B])):
                    out = out.rearrange("c (w s) b -> c w s b", s=2)
                    src = src.rearrange("c (w s b) -> c w s b", s=2, b=B)
                    dve.tensor_copy(out[:, :, 0, :], src[:, :, 0, :])
                    ins = dve.tensor_scalar(out[:, :, 1, :], src[:, :, 1, :], 1.0, None, ALU.add)
                ins.then_inc(d_mod, 1)

            dve.memset(sir[:], 1.0).then_inc(d_set, 1)
            dve.memset(mhalf[:], -0.5)
            dve.memset(hr[REM - 2:REM].bitcast(F32), 1.0)
            dve.memset(onr[REM - 2:REM].bitcast(F32), 1.0)
            dve.wait_ge(q_c, 16 * 9)
            dve.tensor_copy(identb[:], ident[:])
            dve.tensor_copy(maskb[:], maskf[:])
            dve.tensor_scalar(g12[:], gains[:, 0:2], float(C) ** 0.5, None, ALU.mult).then_inc(d_set, 1)
            replicate(0)
            for i in range(NEAR):
                split_chunk(i)
            for l in range(L):
                if l + 1 < L:
                    replicate(l + 1)
                take_mods(l)
            dve.memset(qq[:, 0].rearrange("p s h t -> p (s h t)").bitcast(F32), 0.0).then_inc(d_set, 1)
            dve.wait_ge(d_mod, CR + L)
            dve.wait_ge(q_x0, 16)
            attention(0)
            for i in range(NEAR + len(SPLIT_AT), EARLY):
                split_chunk(i)
            dve.wait_ge(d_ws, CR + EARLY)
            dve.memset(hid[TAIL:TAIL + 1, KT - 1, :], 1.0).then_inc(d_ws, 1)
            mlp(0)
            for l in range(1, L):
                attention(l)
                if l == 1:
                    for i in range(EARLY, len(chunks)):
                        split_chunk(i)
                mlp(l)

        @block.gpsimd
        def _(pool):
            for x in (g_zero, g_set, g_ra, g_rb, g_rc, g_rd, g_rs, g_p3, g_x, g_ew):
                pool.sem_inc(x, CR)

            def norm_factor(l, which, p, n1):
                pool.wait_ge(d_mv, CR + 4 * (n1 + 1))
                pool.wait_ge(d_xn, CR + 4 * (n1 - 1))
                pool.sem_inc(alone, 1)
                r = rstd[:, p, :]
                if l != 2:
                    pool.tensor_scalar(r, mv[:, p, :, 1], LN_EPS, None, ALU.add).then_inc(g_ra, 1)
                    pool.wait_ge(g_ra, CR + n1 + 1)
                    pool.tensor_tensor(r, r, mhalf[:], ALU.pow).then_inc(g_rs, 1)
                    return
                k = n1 - 32
                pool.tensor_tensor(r, mv[:, p, :, 0], mv[:, p, :, 0], ALU.mult).then_inc(g_ra, 1)
                pool.wait_ge(g_ra, CR + n1 + 1)
                pool.tensor_tensor(r, r, mv[:, p, :, 1], ALU.add).then_inc(g_rb, 1)
                pool.wait_ge(g_rb, CR + k + 1)
                pool.sem_inc(alone, 1)
                pool.tensor_scalar(r, r, float(C), RMS_EPS2, ALU.mult, ALU.max).then_inc(g_rc, 1)
                pool.wait_ge(g_rc, CR + k + 1)
                pool.tensor_tensor(r, r, mhalf[:], ALU.pow).then_inc(g_rd, 1)
                pool.wait_ge(g_rd, CR + k + 1)
                pool.sem_inc(alone, 1)
                pool.tensor_scalar(r, r, g12[:, which:which + 1], None, ALU.mult).then_inc(g_rs, 1)

            def part3(l, n):
                for m in range(3):
                    pool.wait_ge(d_p2, CR + 3 * n + m + 1)
                    pool.tensor_tensor(parts[:, m, 2, :], res[:, m % 2, :], parts[:, m, 1, :], ALU.subtract) \
                        .then_inc(g_p3, 1)

            def add_to_x(g, n1):
                for q in range(2):
                    pool.wait_ge(d_gate, CR + 2 * n1 + q + 1)
                    x = X[:, bass.ds(G * g + 2 * q, 2), :]
                    pool.tensor_tensor(x, x, gx[:, q, :, :], ALU.add).then_inc(g_x, 1)

            def attention(l):
                n0, m0 = 8 * l, 16 * l

                def step(g, p, f2, f1):
                    if f2:
                        norm_factor(l, 0, 1 - p, m0 + g + 3)
                    if isinstance(g, int) and g == 6:
                        norm_factor(l, 1, 0, m0 + 8)
                    if f1:
                        part3(l, n0 + g + 2)
                    add_to_x(g, m0 + g)

                for g in range(0 if l == 0 else 1, 2):
                    norm_factor(l, 0, g, m0 + g)
                for g in range(2):
                    part3(l, n0 + g)
                norm_factor(l, 0, 0, m0 + 2)
                with pool.Fori(0, 2) as i:
                    step(2 * i, 0, True, True)
                    step(2 * i + 1, 1, True, True)
                step(4, 0, True, True)
                step(5, 1, False, True)
                step(6, 0, False, False)
                step(7, 1, False, False)

            def mlp(l):
                m0 = 16 * l + 8

                def step(g, p, nxt):
                    if nxt:
                        norm_factor(l, 1, 1 - p, m0 + g + 1)
                    elif l < L - 1:
                        norm_factor(l + 1, 0, 1 - p, m0 + g + 1)
                    if l == 0:
                        pool.wait_ge(d_top, CR + 2 * g + 2)
                        pool.tensor_tensor(cw[:], ebase[:], lg[:], ALU.pow).then_inc(g_ew, 1)
                    add_to_x(g, m0 + g)

                with pool.Fori(0, 3) as i:
                    step(2 * i, 0, True)
                    step(2 * i + 1, 1, True)
                step(6, 0, True)
                step(7, 1, False)

            pool.memset(V[:], 0.0).then_inc(g_zero, 1)
            pool.memset(ebase[:], math.e)
            pool.wait_ge(g_zero, CR + 1)
            ones = V[:].rearrange("t p b v -> t (p b) v")[:, :, 0:H * VS].rearrange("t a (h e) -> t a h e", e=VS)
            pool.memset(ones[:, :, :, D], 1.0).then_inc(g_set, 1)
            for i, r0 in enumerate((32, 96)):
                pool.wait_ge(g_set, CR + i + 1)
                pool.memset(kk[r0:r0 + 32].rearrange("p a h t -> p (a h t)").bitcast(F32), BF16_ONES).then_inc(g_set, 1)
            pool.wait_ge(g_set, CR + 3)
            pool.wait_ge(s_ada, CR + L)
            pool.memset(qq[:, 1].rearrange("p s h t -> p (s h t)").bitcast(F32), 0.0).then_inc(g_set, 1)
            pool.wait_ge(d_set, CR + 2)
            for l in range(L):
                attention(l)
                mlp(l)


class Inputs:
    pass


def kernel(**inputs):
    import numpy as np
    import concourse.bacc as bacc
    from concourse.bass_utils import run_bass_kernel_spmd

    nc = bacc.Bacc("TRN2", target_bir_lowering=False, num_devices=1)
    arrays = {}

    def put(name, a):
        a = np.ascontiguousarray(a)
        arrays["in_" + name] = a
        return nc.dram_tensor("in_" + name, list(a.shape), F32, kind="ExternalInput").ap()

    def given(name, turned=False):
        a = np.asarray(inputs[name])
        return put(name, a.T if turned else a)

    io = Inputs()
    io.x = given("x")
    io.cT = given("cond_1152", turned=True)
    io.ident = put("ident", np.eye(128, dtype=np.float32))
    masks = np.zeros((128, 2), np.float32)
    masks[CR_CH:2 * CR_CH, 0] = masks[3 * CR_CH:4 * CR_CH, 0] = -1.0
    masks[2 * CR_CH:4 * CR_CH, 1] = masks[REM - 1, 1] = -1.0
    io.masks = put("masks", masks)
    own = np.arange(T)[None, :] // H == np.arange(TB)[:, None]
    io.block_mask = put("block_mask", np.stack([np.where(own, 0.0, MASK), own], axis=1).astype(np.float32))
    io.gains = [given("L2_cond_" + x) for x in ("g1", "g2", "qg", "kg")]
    ada = [("L0_cond_w_adaln", "L0_cond_b_adaln"), ("L1_cond_W_ada", "L1_cond_b_ada"),
           ("L2_cond_ada_w", "L2_cond_ada_b"), ("L3_cond_ada_w", "L3_cond_ada_b")]
    qkv = [("L0_cond_w_qkv", "L0_cond_b_qkv"), ("L1_cond_W_qkv", "L1_cond_b_qkv"),
           ("L2_cond_qkv_w", "L2_cond_qkv_b"), ("L3_cond_qkv_w", "L3_cond_qkv_b")]
    proj = [("L0_cond_w_proj", "L0_cond_b_proj"), ("L1_cond_W_proj", "L1_cond_b_proj"),
            ("L2_cond_proj_w", "L2_cond_proj_b"), ("L3_cond_proj_w", "L3_cond_proj_b")]
    fc1 = [("L1_cond_W_fc1", "L1_cond_b_fc1"), ("L2_cond_fc1_w", "L2_cond_fc1_b"), ("L3_cond_fc1_w", "L3_cond_fc1_b")]
    fc2 = [("L1_cond_W_fc2", "L1_cond_b_fc2"), ("L2_cond_fc2_w", "L2_cond_fc2_b"), ("L3_cond_fc2_w", "L3_cond_fc2_b")]

    def by_dim(a, n):
        a = np.asarray(a).reshape(-1, 3, H, D)
        turned = [a[:, i].swapaxes(1, 2) if i < n else a[:, i] for i in range(3)]
        return np.stack([t.reshape(-1, C) for t in turned], axis=1).reshape(-1, 3 * C)

    def pairs(names, turned):
        return [(given(w, turned=(i == turned)), given(b)) for i, (w, b) in enumerate(names)]

    def qkv_pairs(names):
        out = []
        for l, (w, b) in enumerate(names):
            weights = np.asarray(inputs[w])
            out.append((put(w, by_dim(weights.T if l == 2 else weights, 3 if l == 3 else 2)),
                        put(b, by_dim(inputs[b], 3 if l == 3 else 2)[0])))
        return out

    ada, qkv, proj = pairs(ada, 2), qkv_pairs(qkv), pairs(proj, 2)
    fc1, fc2 = pairs(fc1, 1), pairs(fc2, 1)
    w1, b1, w2, b2 = (given("L0_cond_" + x) for x in ("w1", "b1", "w2", "b2"))
    for e in range(E):
        fc1.append((w1[e], b1[e]))
        fc2.append((w2[e], b2[e]))
    io.ada_w, io.ada_b = [w for w, _ in ada], [b for _, b in ada]
    io.qkv_w, io.proj_w = [w for w, _ in qkv], [w for w, _ in proj]
    io.gate_w = given("L0_cond_w_gate")

    def rest(what, k):
        if what == "gate":
            return io.gate_w[CM:C, :], None
        w, b = {"qkv": qkv, "proj": proj, "fc1": fc1}[what][k]
        return w[CM:C, :], b

    io.rest = rest
    io.mlp = lambda k: (fc1[k][0], fc2[k][0], fc2[k][1])
    io.out = nc.dram_tensor("out", [B, T, C], F32, kind="ExternalOutput").ap()
    build(nc, io)
    result = run_bass_kernel_spmd(nc, [arrays], core_ids=[0])
    return result.results[0]["out"]
```
